# Optimizing a Trainium2 kernel written in Bass

```python
import numpy as np
import jax
import jax.numpy as jnp

def _softmax(x, axis=-1):
    return jax.nn.softmax(x, axis=axis)

def _gelu(x):
    return jax.nn.gelu(x, approximate=True)

def _silu(x):
    return jax.nn.silu(x)

def _sigmoid(x):
    return jax.nn.sigmoid(x)

def _layernorm(x, axis=-1, eps=1e-05):
    m = jnp.mean(x, axis=axis, keepdims=True)
    v = jnp.var(x, axis=axis, keepdims=True)
    return (x - m) / jnp.sqrt(v + eps)

def _scatter_add(tgt, idx, src, axis=0):
    return tgt.at[idx].add(src)

def _segment_sum(src, seg, n):
    return jax.ops.segment_sum(src, seg, n)
kernel_name = 'mk_rec_standalone_d1_rec_r8_645f4d'

def setup_inputs(seed: int=0):
    np.random.seed(seed)
    _w = jnp.asarray

    def _rec_inputs():
        import jax
        import jax.numpy as jnp
        _rk = jax.random.key(seed)
        r_dense_x = 8.7408e-05 + 1.0001 * jax.random.normal(jax.random.fold_in(_rk, 1), (512, 13), jnp.float32)
        r_sparse_x = jnp.stack([jax.random.randint(jax.random.fold_in(jax.random.fold_in(_rk, 2), 0), (512,), 0, 49999, jnp.int32), jax.random.randint(jax.random.fold_in(jax.random.fold_in(_rk, 2), 1), (512,), 0, 6250, jnp.int32), jax.random.randint(jax.random.fold_in(jax.random.fold_in(_rk, 2), 2), (512,), 0, 6250, jnp.int32), jax.random.randint(jax.random.fold_in(jax.random.fold_in(_rk, 2), 3), (512,), 0, 49998, jnp.int32), jax.random.randint(jax.random.fold_in(jax.random.fold_in(_rk, 2), 4), (512,), 1, 49999, jnp.int32), jax.random.randint(jax.random.fold_in(jax.random.fold_in(_rk, 2), 5), (512,), 1, 6250, jnp.int32), jax.random.randint(jax.random.fold_in(jax.random.fold_in(_rk, 2), 6), (512,), 0, 49995, jnp.int32), jax.random.randint(jax.random.fold_in(jax.random.fold_in(_rk, 2), 7), (512,), 1, 6250, jnp.int32), jax.random.randint(jax.random.fold_in(jax.random.fold_in(_rk, 2), 8), (512,), 0, 6250, jnp.int32), jax.random.randint(jax.random.fold_in(jax.random.fold_in(_rk, 2), 9), (512,), 3, 49999, jnp.int32), jax.random.randint(jax.random.fold_in(jax.random.fold_in(_rk, 2), 10), (512,), 2, 49998, jnp.int32), jax.random.randint(jax.random.fold_in(jax.random.fold_in(_rk, 2), 11), (512,), 0, 49997, jnp.int32), jax.random.randint(jax.random.fold_in(jax.random.fold_in(_rk, 2), 12), (512,), 0, 6250, jnp.int32), jax.random.randint(jax.random.fold_in(jax.random.fold_in(_rk, 2), 13), (512,), 0, 49999, jnp.int32), jax.random.randint(jax.random.fold_in(jax.random.fold_in(_rk, 2), 14), (512,), 1, 49994, jnp.int32), jax.random.randint(jax.random.fold_in(jax.random.fold_in(_rk, 2), 15), (512,), 2, 6250, jnp.int32), jax.random.randint(jax.random.fold_in(jax.random.fold_in(_rk, 2), 16), (512,), 1, 6250, jnp.int32), jax.random.randint(jax.random.fold_in(jax.random.fold_in(_rk, 2), 17), (512,), 0, 6250, jnp.int32), jax.random.randint(jax.random.fold_in(jax.random.fold_in(_rk, 2), 18), (512,), 1, 6250, jnp.int32), jax.random.randint(jax.random.fold_in(jax.random.fold_in(_rk, 2), 19), (512,), 0, 49998, jnp.int32), jax.random.randint(jax.random.fold_in(jax.random.fold_in(_rk, 2), 20), (512,), 1, 6250, jnp.int32), jax.random.randint(jax.random.fold_in(jax.random.fold_in(_rk, 2), 21), (512,), 1, 49997, jnp.int32), jax.random.randint(jax.random.fold_in(jax.random.fold_in(_rk, 2), 22), (512,), 3, 49998, jnp.int32), jax.random.randint(jax.random.fold_in(jax.random.fold_in(_rk, 2), 23), (512,), 2, 6250, jnp.int32), jax.random.randint(jax.random.fold_in(jax.random.fold_in(_rk, 2), 24), (512,), 2, 6250, jnp.int32), jax.random.randint(jax.random.fold_in(jax.random.fold_in(_rk, 2), 25), (512,), 2, 49998, jnp.int32)], axis=1)
        return (r_dense_x, r_sparse_x)
    r_dense_x, r_sparse_x = _rec_inputs()

    def _L0_rec_setup():
        import jax, jax.numpy as jnp
        import numpy as np
        N_FEAT = 27
        LI = np.array([i for i in range(N_FEAT) for j in range(i)])
        LJ = np.array([j for i in range(N_FEAT) for j in range(i)])

        def _mlp(x, Ws, bs):
            for W, b in zip(Ws, bs):
                x = jax.nn.relu(x @ W + b)
            return x
        key = jax.random.key(seed)
        ks = jax.random.split(key, 32)
        B, V, D = (4096, 6250, 128)
        bot = [13, 512, 256, 128]
        top = [479, 1024, 1024, 512, 256, 1]
        inp = {'dense_x': jax.random.normal(ks[0], (B, 13), dtype=jnp.float32), 'sparse_x': jax.random.randint(ks[1], (B, 26), 0, V, dtype=jnp.int64), 'emb': jax.random.normal(ks[2], (26, V, D), dtype=jnp.float32) * 0.01}
        for i in range(3):
            inp[f'bw{i}'] = jax.random.normal(ks[3 + i], (bot[i], bot[i + 1]), dtype=jnp.float32) * (1.0 / np.sqrt(bot[i]))
            inp[f'bb{i}'] = jnp.zeros((bot[i + 1],), dtype=jnp.float32)
        for i in range(5):
            inp[f'tw{i}'] = jax.random.normal(ks[8 + i], (top[i], top[i + 1]), dtype=jnp.float32) * (1.0 / np.sqrt(top[i]))
            inp[f'tb{i}'] = jnp.zeros((top[i + 1],), dtype=jnp.float32)
        return inp
    _L0_rec_all = _L0_rec_setup()
    _L0_rec_in = {k: v for k, v in _L0_rec_all.items() if k in ('emb', 'bw0', 'bb0', 'bw1', 'bb1', 'bw2', 'bb2', 'tw0', 'tb0', 'tw1', 'tb1', 'tw2', 'tb2', 'tw3', 'tb3', 'tw4', 'tb4')}
    del _L0_rec_all
    return {'r_dense_x': r_dense_x, 'r_sparse_x': r_sparse_x, 'L0_rec_emb': _L0_rec_in['emb'], 'L0_rec_bw0': _L0_rec_in['bw0'], 'L0_rec_bb0': _L0_rec_in['bb0'], 'L0_rec_bw1': _L0_rec_in['bw1'], 'L0_rec_bb1': _L0_rec_in['bb1'], 'L0_rec_bw2': _L0_rec_in['bw2'], 'L0_rec_bb2': _L0_rec_in['bb2'], 'L0_rec_tw0': _L0_rec_in['tw0'], 'L0_rec_tb0': _L0_rec_in['tb0'], 'L0_rec_tw1': _L0_rec_in['tw1'], 'L0_rec_tb1': _L0_rec_in['tb1'], 'L0_rec_tw2': _L0_rec_in['tw2'], 'L0_rec_tb2': _L0_rec_in['tb2'], 'L0_rec_tw3': _L0_rec_in['tw3'], 'L0_rec_tb3': _L0_rec_in['tb3'], 'L0_rec_tw4': _L0_rec_in['tw4'], 'L0_rec_tb4': _L0_rec_in['tb4']}

def reference(r_dense_x, r_sparse_x, L0_rec_emb, L0_rec_bw0, L0_rec_bb0, L0_rec_bw1, L0_rec_bb1, L0_rec_bw2, L0_rec_bb2, L0_rec_tw0, L0_rec_tb0, L0_rec_tw1, L0_rec_tb1, L0_rec_tw2, L0_rec_tb2, L0_rec_tw3, L0_rec_tb3, L0_rec_tw4, L0_rec_tb4):
    import jax
    import jax.numpy as jnp

    def _L0_rec_ref(dense_x, sparse_x, emb, bw0, bb0, bw1, bb1, bw2, bb2, tw0, tb0, tw1, tb1, tw2, tb2, tw3, tb3, tw4, tb4):
        import jax, jax.numpy as jnp
        import numpy as np
        N_FEAT = 27
        LI = np.array([i for i in range(N_FEAT) for j in range(i)])
        LJ = np.array([j for i in range(N_FEAT) for j in range(i)])

        def _mlp(x, Ws, bs):
            for W, b in zip(Ws, bs):
                x = jax.nn.relu(x @ W + b)
            return x
        B = dense_x.shape[0]
        bot_out = _mlp(dense_x, [bw0, bw1, bw2], [bb0, bb1, bb2])
        gathered = jnp.take_along_axis(emb[None, :, :, :], sparse_x.T[None, :, :, None].astype(jnp.int32) * 0, 0) if False else jnp.stack([emb[t][sparse_x[:, t]] for t in range(emb.shape[0])], axis=1)
        features = jnp.concatenate([bot_out[:, None, :], gathered], axis=1)
        Z = jnp.einsum('bnd,bmd->bnm', features, features)
        interact = Z[:, LI, LJ]
        x = jnp.concatenate([bot_out, interact], axis=1)
        return _mlp(x, [tw0, tw1, tw2, tw3, tw4], [tb0, tb1, tb2, tb3, tb4])
    y = _L0_rec_ref(r_dense_x, r_sparse_x, L0_rec_emb, L0_rec_bw0, L0_rec_bb0, L0_rec_bw1, L0_rec_bb1, L0_rec_bw2, L0_rec_bb2, L0_rec_tw0, L0_rec_tb0, L0_rec_tw1, L0_rec_tb1, L0_rec_tw2, L0_rec_tb2, L0_rec_tw3, L0_rec_tb3, L0_rec_tw4, L0_rec_tb4)
    return y

_drawn_inputs = setup_inputs


def setup_inputs(seed=0):
    import zlib

    import numpy as np

    out = dict(_drawn_inputs(seed))
    spreads = {'L0_rec_bb0': (0.0, 0.282),
     'L0_rec_bb1': (0.0, 0.268),
     'L0_rec_bb2': (0.0, 0.1),
     'L0_rec_tb0': (0.0, 0.1),
     'L0_rec_tb1': (0.0, 0.1),
     'L0_rec_tb2': (0.0, 0.1),
     'L0_rec_tb3': (0.0, 0.1)}
    factors = {'L0_rec_emb': 4.327}
    for name, (base, spread) in spreads.items():
        noise = np.random.default_rng([zlib.crc32(name.encode()), seed]).standard_normal(out[name].shape)
        drawn = base * np.exp(spread * noise) if base else spread * noise
        out[name] = jnp.asarray(drawn.astype(out[name].dtype))
    for name, factor in factors.items():
        out[name] = (out[name] * factor).astype(out[name].dtype)
    return out
```

```python
from contextlib import ExitStack

import numpy as np
import concourse.bass as bass
from concourse import mybir
from concourse.alu_op_type import AluOpType as ALU

F32 = mybir.dt.float32
F32R = mybir.dt.float32r
I32 = mybir.dt.int32
U32 = mybir.dt.uint32
ACT = mybir.ActivationFunctionType

P = 128
BATCH, DENSE = 512, 13
CHUNKS = BATCH // P
TABLES, VOCAB, DIM = 26, 6250, 128
FEATS = TABLES + 1
SLOT = 32
LOT = 4
LOTS = -(-TABLES // LOT)
ACT_LOTS = (LOTS + 1) // 2
DVE_LOTS = LOTS // 2
GROUP = 4
BANK_GROUPS = 4
Z_BANKS = P // (GROUP * BANK_GROUPS)
HOPS = (FEATS - 1) // 2
PAIR_TILES = 3
PAIR_ROWS = FEATS * HOPS // PAIR_TILES
WRAP = FEATS + HOPS
BOT_TILE = PAIR_TILES
B0, B1, B2 = 512, 256, 128
T0, T1, T2, T3 = 1024, 1024, 512, 256
NB = 512
STAGES = 3


def pair_row_table():
    table = np.zeros((PAIR_ROWS, PAIR_TILES), np.uint32)
    for i in range(PAIR_TILES):
        for p in range(PAIR_ROWS):
            n = i * (FEATS // PAIR_TILES) + p // HOPS
            m = (n + p % HOPS + 1) % FEATS
            a, b = max(n, m), min(n, m)
            table[p, i] = DIM + a * (a - 1) // 2 + b
    return table


def flat(ap, offset, dims):
    return bass.AP(tensor=ap.tensor, offset=offset, ap=dims)


def after(eng, sem, count):
    if not isinstance(count, int) or count > 0:
        eng.wait_ge(sem, count)


def rec_kernel(nc, dense, sparse, emb, bw, bb, tw, tb, pair_rows, scratch, out):
    with ExitStack() as ctx:
        def sb(name, shape, dt=F32, scope=ctx):
            return scope.enter_context(nc.sbuf_tensor(name, shape, dt))

        def sem(name):
            return ctx.enter_context(nc.semaphore(name))

        w0h = sb("w0h", [P, PAIR_TILES + 1, T0], F32R)
        w0l = sb("w0l", [P, PAIR_TILES + 1, T0], F32R)
        w1h = sb("w1h", [P, T0 // P, T1], F32R)
        w1l = sb("w1l", [P, T0 // P, T1], F32R)
        w2h = sb("w2h", [P, T1 // P, T2], F32R)
        w2l = sb("w2l", [P, T1 // P, T2], F32R)
        w3 = sb("w3", [P, T2 // P, T3])
        w4 = sb("w4", [P, T3 // P])
        bias1 = sb("bias1", [P, T1])
        bias2 = sb("bias2", [P, T2])
        bias3 = sb("bias3", [P, T3 // P])
        bias4 = sb("bias4", [1, 1])
        ident = sb("ident", [P, P])
        botT = sb("botT", [P, BATCH])
        rows = sb("rows", [P, TABLES, DIM])
        featT = sb("featT", [P, P, SLOT])
        pairs = sb("pairs", [P, PAIR_TILES, P])
        index_raw = sb("index_raw", [P, CHUNKS, TABLES], I32)
        index_tmp = sb("index_tmp", [P, CHUNKS, TABLES])
        index_base = sb("index_base", [P, CHUNKS, TABLES], I32)
        index = sb("index", [P, CHUNKS, TABLES], U32)
        pair_index = sb("pair_index", [PAIR_ROWS, PAIR_TILES], U32)

        with ExitStack() as early:
            x0 = sb("x0", [P, CHUNKS, DENSE], F32, early)
            x0T = sb("x0T", [DENSE, BATCH], F32, early)
            v0 = sb("v0", [DENSE, B0], F32, early)
            v1 = sb("v1", [P, B0 // P, B1], F32, early)
            v2 = sb("v2", [P, B1 // P, B2], F32, early)
            c0 = sb("c0", [P, B0 // P], F32, early)
            c1 = sb("c1", [P, B1 // P], F32, early)
            c2 = sb("c2", [P, 1], F32, early)
            h0T = sb("h0T", [P, B0 // P, BATCH], F32, early)
            h1T = sb("h1T", [P, B1 // P, BATCH], F32, early)
        dots = sb("dots", [FEATS, FEATS, P])
        y_evac = sb("y_evac", [P, 2, NB])
        y2T = sb("y2T", [P, T2 // P, P])
        y3T = sb("y3T", [P, T3 // P, P])
        out_row = sb("out_row", [1, BATCH])
        with ExitStack() as early:
            stage = sb("stage", [P, STAGES, 1024], F32, early)
        xh = sb("xh", [P, PAIR_TILES + 1, P], F32R)
        xl = sb("xl", [P, PAIR_TILES + 1, P], F32R)
        yh = sb("yh", [P, 2, NB], F32R)
        yl = sb("yl", [P, 2, NB], F32R)

        def bank(name):
            return ctx.enter_context(nc.psum_tensor(name, [P, NB], F32))

        acc = [bank("acc0"), bank("acc1"), bank("acc2")]
        turned = [bank("turned0"), bank("turned1")]
        fz = [bank("fz0"), bank("fz1")]
        last = bank("last")

        s_sparse, s_dense, s_pidx, s_botw, s_topw, s_one = map(
            sem, ("sparse_in", "dense_in", "pair_index_in", "bottom_weights_in", "top_small_in", "ones_set"))
        s_base, s_ident0, s_ident, s_chain, s_index, s_pad = map(
            sem, ("index_base_set", "ident_zero", "ident_set", "index_chain", "index_ready", "pad_set"))
        s_stage = [sem(f"staged{i}") for i in range(STAGES)]
        s_pair = [sem(f"pair_weights_in{i}") for i in range(PAIR_TILES)]
        s_brow = sem("bias_row_in")
        s_wh, s_wl = sem("weight_hi"), sem("weight_lo")
        s_x0t, s_x0, s_l0b, s_h0, s_l1b, s_h1, s_l2b, s_bot = map(
            sem, ("x0_turned", "x0T_ready", "bot0_done", "h0_ready", "bot1_done", "h1_ready", "bot2_done",
                  "botT_ready"))
        s_gather = [sem(f"gathered{j}") for j in range(LOTS)]
        s_ft, s_fa, s_fd, s_fb = map(sem, ("lot_turned", "lot_copied_act", "lot_copied_dve", "bot_feature_copied"))
        s_z, s_za, s_zd = map(sem, ("dots_done", "dots_copied_act", "dots_copied_dve"))
        s_scr, s_pin = sem("scratch_written"), sem("pairs_in")
        s_xhb, s_xlb, s_xhp, s_xlp = map(sem, ("bot_hi", "bot_lo", "pairs_hi", "pairs_lo"))
        s_l = [sem(f"layer{i}_done") for i in range(5)]
        s_e = [sem(f"layer{i}_copied") for i in range(3)]
        s_t = [sem(f"layer{i}_turned") for i in range(3)]
        s_yh = [sem(f"layer{i}_hi") for i in range(2)]
        s_yl = [sem(f"layer{i}_lo") for i in range(2)]
        s_y2, s_y3, s_y4, s_out = map(sem, ("y2T_ready", "y3T_ready", "out_ready", "out_written"))

        def pair_piece(i):
            k = PAIR_ROWS + (i == PAIR_TILES - 1)
            return w0h[0:k, i, :], w0l[0:k, i, :], k

        pieces = [(w0h[:, BOT_TILE, :], w0l[:, BOT_TILE, :], P)]
        sources = [tw[0][0:P, :]]
        for k in range(T0 // P):
            pieces.append((w1h[:, k, :], w1l[:, k, :], P))
            sources.append(tw[1][k * P:(k + 1) * P, :])
        for k in range(0, T1 // P, 2):
            pieces.append((w2h[:, k:k + 2, :].rearrange("p k n -> p (k n)"),
                           w2l[:, k:k + 2, :].rearrange("p k n -> p (k n)"), P))
            sources.append(tw[2][k * P:(k + 2) * P, :].rearrange("(k p) n -> p k n", p=P))
        direct = len(pieces)
        pieces += [pair_piece(i) for i in range(PAIR_TILES)]
        total = len(pieces)

        def piece_in(eng, n):
            if n < direct:
                eng.wait_ge(s_stage[n % STAGES], 16 * (n // STAGES + 1))
            else:
                eng.wait_ge(s_pair[n - direct], 16)
            if n == total - 1:
                eng.wait_ge(s_brow, 16)

        def dot_quadrant(z, s):
            at = z * GROUP * BANK_GROUPS + s
            to = dots[:, :, at:at + GROUP * (BANK_GROUPS - 1) + 1:GROUP].rearrange("n m g -> n g m")
            block_ = fz[z % 2][SLOT * s:SLOT * s + FEATS, 0:BANK_GROUPS * GROUP * FEATS]
            return to, block_.rearrange("n (g c) -> n g c", g=BANK_GROUPS)[:, :, s * FEATS:(s + 1) * FEATS]

        block = ctx.enter_context(nc.Block())

        @block.sync
        def _(sp):
            sp.dma_start(index_raw[:], sparse.rearrange("(c p) t -> p c t", p=P)).then_inc(s_sparse, 16)
            sp.dma_start(x0[:], dense.rearrange("(c p) d -> p c d", p=P)).then_inc(s_dense, 16)
            sp.dma_start(v0[:], bw[0]).then_inc(s_botw, 16)

            def load_piece(n):
                after(sp, s_wl, n - STAGES + 1)
                dst = stage[:, n % STAGES, :]
                if len(sources[n].shape) == 3:
                    dst = dst.rearrange("p (k n) -> p k n", k=2)
                sp.dma_start(dst, sources[n]).then_inc(s_stage[n % STAGES], 16)

            sp.dma_start(v1[:], bw[1].rearrange("(k p) n -> p k n", p=P)).then_inc(s_botw, 16)
            load_piece(0)
            sp.dma_start(v2[:], bw[2].rearrange("(k p) n -> p k n", p=P)).then_inc(s_botw, 16)
            load_piece(1)
            load_piece(2)
            sp.dma_start(pair_index[:], pair_rows).then_inc(s_pidx, 16)
            sp.dma_start(w3[:], tw[3].rearrange("(k p) n -> p k n", p=P)).then_inc(s_topw, 16)
            sp.dma_start(w4[:], tw[4].rearrange("(k p) n -> p (k n)", p=P), allow_slow_non_contiguous=True).then_inc(s_topw, 16)
            sp.dma_start(bias1[:], flat(tb[1], 0, [[0, P], [1, T1]])).then_inc(s_topw, 16)
            sp.dma_start(bias2[:], flat(tb[2], 0, [[0, P], [1, T2]])).then_inc(s_topw, 16)
            for n in range(STAGES, direct):
                load_piece(n)
            sp.wait_ge(s_wl, total - STAGES)
            sp.dma_start(stage[PAIR_ROWS:PAIR_ROWS + 1, (total - 1) % STAGES, :],
                         tb[0].rearrange("(o n) -> o n", o=1)).then_inc(s_brow, 16)

            def regroup(c):
                sp.wait_ge(s_za, Z_BANKS * (c + 1))
                sp.wait_ge(s_zd, Z_BANKS * (c + 1))
                after(sp, s_pin, 16 * PAIR_TILES * c)
                sp.dma_start(scratch[:, 0:FEATS, :], dots[:]).then_inc(s_scr, 16)
                sp.dma_start(scratch[:, FEATS:WRAP, :], dots[:, 0:HOPS, :]).then_inc(s_scr, 16)
                sp.wait_ge(s_scr, 32 * (c + 1))
                after(sp, s_xlp, c)
                if isinstance(c, int) and c == 0:
                    sp.wait_ge(s_one, 1)
                for i in range(PAIR_TILES):
                    tile_feats = FEATS // PAIR_TILES
                    src = flat(scratch, (i * tile_feats * (WRAP + 1) + 1) * P,
                               [[(WRAP + 1) * P, tile_feats], [P, HOPS], [1, P]])
                    sp.dma_start(pairs[0:PAIR_ROWS, i, :], src).then_inc(s_pin, 16)

            for c in range(CHUNKS):
                regroup(c)
            sp.wait_ge(s_y4, CHUNKS)
            sp.dma_start(out.rearrange("b o -> o b"), out_row[:]).then_inc(s_out, 16)
            sp.wait_ge(s_out, 16)

        @block.gpsimd
        def _(pool):
            pool.iota(index_base[:], pattern=[[0, CHUNKS], [VOCAB, TABLES]], base=0,
                      channel_multiplier=0).then_inc(s_base, 1)
            pool.memset(ident[:], 0.0).then_inc(s_ident0, 1)
            pool.wait_ge(s_ident0, 1)
            pool.affine_select(out=ident[:], in_=ident[:], compare_op=ALU.not_equal, fill=1.0, base=0,
                               pattern=[[-1, P]], channel_multiplier=1).then_inc(s_ident, 1)
            table = emb.rearrange("t v d -> (t v) d")

            def gather_chunk(c):
                for t in range(TABLES):
                    if t % LOT == 0:
                        after(pool, s_ft, LOTS * (c - 1) + t // LOT + 1)
                    pool.indirect_dma_start(
                        rows[:, t, :], None, table,
                        bass.IndirectOffsetOnAxis(ap=index[:, c, t:t + 1], axis=0)).then_inc(s_gather[t // LOT], 16)

            pool.wait_ge(s_index, 1)
            gather_chunk(0)
            pool.wait_ge(s_pidx, 16)
            for i in range(PAIR_TILES):
                n = direct + i
                pool.wait_ge(s_wl, n - STAGES + 1)
                pool.indirect_dma_start(
                    stage[0:PAIR_ROWS, n % STAGES, :], None, tw[0],
                    bass.IndirectOffsetOnAxis(ap=pair_index[:, i:i + 1], axis=0)).then_inc(s_pair[i], 16)
            for c in range(1, CHUNKS):
                gather_chunk(c)

        @block.scalar
        def _(act):
            act.dma_start(c0[:], bb[0].rearrange("(k p) -> p k", p=P), allow_slow_non_contiguous=True).then_inc(s_botw, 16)
            act.dma_start(c1[:], bb[1].rearrange("(k p) -> p k", p=P), allow_slow_non_contiguous=True).then_inc(s_botw, 16)
            act.dma_start(c2[:], bb[2].rearrange("(k p) -> p k", p=P), allow_slow_non_contiguous=True).then_inc(s_botw, 16)
            act.dma_start(bias3[:], tb[3].rearrange("(k p) -> p k", p=P), allow_slow_non_contiguous=True).then_inc(s_topw, 16)
            act.dma_start(bias4[:], tb[4].rearrange("(o n) -> o n", o=1)).then_inc(s_topw, 16)

            def weight_hi(n):
                hi, _, k = pieces[n]
                piece_in(act, n)
                nc.scalar.copy(hi, stage[0:k, n % STAGES, :]).then_inc(s_wh, 1)

            def feature_lot(c, j):
                act.wait_ge(s_ft, LOTS * c + j + 1)
                w = min(LOT, TABLES - LOT * j)
                nc.scalar.copy(
                    featT[:, :, 1 + LOT * j:1 + LOT * j + w].rearrange("d b n -> d n b"),
                    fz[j % 2][:, 0:w * P].rearrange("d (n b) -> d n b", b=P)).then_inc(s_fa, 1)

            def dots_out(c):
                after(act, s_scr, 32 * c)
                for z in range(Z_BANKS):
                    act.wait_ge(s_z, Z_BANKS * c + z + 1)
                    for s in (0, 1):
                        ins = nc.scalar.copy(*dot_quadrant(z, s))
                    ins.then_inc(s_za, 1)

            def split_hi(layer, c, half):
                act.wait_ge(s_t[layer], 2 * c + half + 1)
                nc.scalar.activation(yh[:, half, :], turned[half][:], ACT.Relu).then_inc(s_yh[layer], 1)

            def bot_hi(c):
                after(act, s_l[0], 2 * c)
                nc.scalar.copy(xh[:, BOT_TILE, :], botT[:, c * P:(c + 1) * P]).then_inc(s_xhb, 1)

            def pairs_hi(c):
                act.wait_ge(s_pin, 16 * PAIR_TILES * (c + 1))
                after(act, s_l[0], 2 * c)
                nc.scalar.copy(xh[0:PAIR_ROWS + 1, 0:PAIR_TILES, :],
                               pairs[0:PAIR_ROWS + 1, :, :]).then_inc(s_xhp, 1)

            def layer2_out(c):
                act.wait_ge(s_t[2], c + 1)
                nc.scalar.activation(y2T[:].rearrange("p k b -> p (k b)"), turned[0][:],
                                     ACT.Relu).then_inc(s_y2, 1)

            def layer3_out(c):
                act.wait_ge(s_l[3], c + 1)
                for o in range(T3 // P):
                    ins = nc.scalar.activation(y3T[:, o, :], last[:, o * P:(o + 1) * P], ACT.Relu,
                                               bias=bias3[:, o:o + 1])
                ins.then_inc(s_y3, 1)

            def layer4_out(c):
                act.wait_ge(s_l[4], c + 1)
                nc.scalar.activation(out_row[0:1, c * P:(c + 1) * P], last[0:1, T3:T3 + P], ACT.Relu,
                                     bias=bias4[:]).then_inc(s_y4, 1)

            act.wait_ge(s_x0t, 1)
            nc.scalar.copy(x0T[:], turned[1][0:DENSE, :]).then_inc(s_x0, 1)
            act.wait_ge(s_botw, 6 * 16)
            for o in range(B0 // P):
                act.wait_ge(s_l0b, o + 1)
                nc.scalar.activation(h0T[:, o, :], (acc + [last])[o][:], ACT.Relu,
                                     bias=c0[:, o:o + 1]).then_inc(s_h0, 1)
            for o in range(B1 // P):
                act.wait_ge(s_l1b, o + 1)
                nc.scalar.activation(h1T[:, o, :], turned[o][:], ACT.Relu, bias=c1[:, o:o + 1]).then_inc(s_h1, 1)
            act.wait_ge(s_l2b, 1)
            nc.scalar.activation(botT[:], acc[0][:], ACT.Relu, bias=c2[:]).then_inc(s_bot, 1)
            act.wait_ge(s_pad, 1)
            lot = 0
            for n in range(direct):
                weight_hi(n)
                if n in (4, 7, 10):
                    feature_lot(0, lot)
                    lot += 2
            feature_lot(0, lot)
            act.wait_ge(s_topw, 6 * 16)

            def chunk(c):
                first = isinstance(c, int) and c == 0
                end = isinstance(c, int) and c == CHUNKS - 1
                if not first:
                    bot_hi(c)
                dots_out(c)
                if first:
                    for n in range(direct, total):
                        weight_hi(n)
                    act.wait_ge(s_wl, total)
                    bot_hi(c)
                else:
                    split_hi(1, c - 1, 1)
                    layer2_out(c - 1)
                pairs_hi(c)
                if not first:
                    layer3_out(c - 1)
                split_hi(0, c, 0)
                if not first:
                    layer4_out(c - 1)
                split_hi(0, c, 1)
                if not end:
                    for j in range(0, LOTS, 2):
                        feature_lot(c + 1, j)
                split_hi(1, c, 0)

            for c in range(CHUNKS):
                chunk(c)
            split_hi(1, CHUNKS - 1, 1)
            layer2_out(CHUNKS - 1)
            layer3_out(CHUNKS - 1)
            layer4_out(CHUNKS - 1)

        @block.vector
        def _(dve):
            nc.vector.memset(featT[:, :, FEATS:SLOT], 0.0).then_inc(s_pad, 1)
            nc.vector.memset(pairs[96:P, :, :], 1.0).then_inc(s_one, 1)
            dve.wait_ge(s_sparse, 16)
            nc.vector.tensor_scalar(index_tmp[:], index_raw[:], 0.0, float(VOCAB), ALU.is_lt,
                                    ALU.mult).then_inc(s_chain, 1)
            dve.wait_ge(s_chain, 1)
            nc.vector.tensor_tensor(index_tmp[:], index_tmp[:], index_raw[:], ALU.add).then_inc(s_chain, 1)
            dve.wait_ge(s_chain, 2)
            nc.vector.tensor_scalar(index_tmp[:], index_tmp[:], 0.0, float(VOCAB - 1), ALU.max,
                                    ALU.min).then_inc(s_chain, 1)
            dve.wait_ge(s_chain, 3)
            dve.wait_ge(s_base, 1)
            nc.vector.tensor_tensor(index[:], index_tmp[:], index_base[:], ALU.add).then_inc(s_index, 1)

            def weight_lo(n):
                hi, lo, k = pieces[n]
                dve.wait_ge(s_wh, n + 1)
                nc.vector.tensor_tensor(lo, stage[0:k, n % STAGES, :], hi.bitcast(F32),
                                        ALU.subtract).then_inc(s_wl, 1)

            def feature_lot(c, j):
                dve.wait_ge(s_ft, LOTS * c + j + 1)
                nc.vector.tensor_copy(
                    featT[:, :, 1 + LOT * j:1 + LOT * (j + 1)].rearrange("d b n -> d n b"),
                    fz[j % 2][:].rearrange("d (n b) -> d n b", b=P)).then_inc(s_fd, 1)

            def bot_feature(c):
                dve.wait_ge(s_ft, LOTS * c + 1)
                nc.vector.tensor_copy(featT[:, :, 0], botT[:, c * P:(c + 1) * P]).then_inc(s_fb, 1)

            def dots_out(c):
                after(dve, s_scr, 32 * c)
                for z in range(Z_BANKS):
                    dve.wait_ge(s_z, Z_BANKS * c + z + 1)
                    for s in (2, 3):
                        ins = nc.vector.tensor_copy(*dot_quadrant(z, s))
                    ins.then_inc(s_zd, 1)

            def bot_lo(c):
                dve.wait_ge(s_xhb, c + 1)
                nc.vector.tensor_tensor(xl[:, BOT_TILE, :], botT[:, c * P:(c + 1) * P],
                                        xh[:, BOT_TILE, :].bitcast(F32), ALU.subtract).then_inc(s_xlb, 1)

            def pairs_lo(c):
                dve.wait_ge(s_xhp, c + 1)
                nc.vector.tensor_tensor(xl[0:PAIR_ROWS + 1, 0:PAIR_TILES, :], pairs[0:PAIR_ROWS + 1, :, :],
                                        xh[0:PAIR_ROWS + 1, 0:PAIR_TILES, :].bitcast(F32),
                                        ALU.subtract).then_inc(s_xlp, 1)

            def copy_out(layer, c, half):
                if layer == 2:
                    dve.wait_ge(s_l[2], c + 1)
                    nc.vector.tensor_tensor(y_evac[:, 0, :], acc[2][:], bias2[:], ALU.add).then_inc(s_e[2], 1)
                    return
                dve.wait_ge(s_l[layer], 2 * c + half + 1)
                if layer == 0:
                    ins = nc.vector.tensor_copy(y_evac[:, half, :], acc[half][:])
                else:
                    ins = nc.vector.tensor_tensor(y_evac[:, half, :], acc[half][:],
                                                  bias1[:, half * NB:(half + 1) * NB], ALU.add)
                ins.then_inc(s_e[layer], 1)

            def split_lo(layer, c, half):
                dve.wait_ge(s_yh[layer], 2 * c + half + 1)
                nc.vector.scalar_tensor_tensor(out=yl[:, half, :], in0=turned[half][:], scalar=0.0,
                                               in1=yh[:, half, :].bitcast(F32), op0=ALU.max,
                                               op1=ALU.subtract).then_inc(s_yl[layer], 1)

            lot = 1
            for n in range(direct):
                weight_lo(n)
                if n in (5, 8, 11):
                    feature_lot(0, lot)
                    lot += 2
                if n == 2:
                    dve.wait_ge(s_bot, 1)
            bot_feature(0)
            dve.wait_ge(s_topw, 6 * 16)

            def chunk(c):
                first = isinstance(c, int) and c == 0
                end = isinstance(c, int) and c == CHUNKS - 1
                if not first:
                    bot_lo(c)
                dots_out(c)
                if first:
                    for n in range(direct, total):
                        weight_lo(n)
                    bot_lo(c)
                else:
                    split_lo(1, c - 1, 1)
                    copy_out(2, c - 1, 0)
                pairs_lo(c)
                for half in range(2):
                    copy_out(0, c, half)
                    split_lo(0, c, half)
                if not end:
                    for j in range(1, LOTS, 2):
                        feature_lot(c + 1, j)
                    bot_feature(c + 1)
                copy_out(1, c, 0)
                split_lo(1, c, 0)
                copy_out(1, c, 1)

            for c in range(CHUNKS):
                chunk(c)
            split_lo(1, CHUNKS - 1, 1)
            copy_out(2, CHUNKS - 1, 0)

        @block.tensor
        def _(pe):
            def turn_lot(c, j):
                w = min(LOT, TABLES - LOT * j)
                pe.wait_ge(s_gather[j], 16 * w * (c + 1))
                if j < 2:
                    after(pe, s_za, Z_BANKS * c)
                    after(pe, s_zd, Z_BANKS * c)
                elif j % 2 == 0:
                    pe.wait_ge(s_fa, ACT_LOTS * c + j // 2)
                else:
                    pe.wait_ge(s_fd, DVE_LOTS * c + j // 2)
                for i in range(w):
                    ins = nc.tensor.transpose(fz[j % 2][:, i * P:(i + 1) * P], rows[:, LOT * j + i, :], ident[:])
                ins.then_inc(s_ft, 1)

            def dots_of(c):
                pe.wait_ge(s_fa, ACT_LOTS * (c + 1))
                pe.wait_ge(s_fd, DVE_LOTS * (c + 1))
                pe.wait_ge(s_fb, c + 1)
                for z in range(Z_BANKS):
                    if z >= 2:
                        pe.wait_ge(s_za, Z_BANKS * c + z - 1)
                        pe.wait_ge(s_zd, Z_BANKS * c + z - 1)
                    for g in range(BANK_GROUPS):
                        b = (z * BANK_GROUPS + g) * GROUP
                        w = GROUP * FEATS
                        ins = nc.tensor.matmul(
                            fz[z % 2][:, g * w:(g + 1) * w].rearrange("n (s m) -> n s m", s=GROUP),
                            featT[:, b:b + GROUP, :].rearrange("d s n -> d (s n)"),
                            featT[:, b:b + GROUP, 0:FEATS], start=True, stop=True)
                    ins.then_inc(s_z, 1)

            def product(dst, ah, al, wh, wl, first, end):
                nc.tensor.matmul(dst, ah, wh, start=first, stop=False)
                nc.tensor.matmul(dst, ah, wl, start=False, stop=False)
                return nc.tensor.matmul(dst, al, wh, start=False, stop=end)

            def layer0(c, half, k, first=False, end=False):
                n = P if k == BOT_TILE else PAIR_ROWS + (k == PAIR_TILES - 1)
                cols = slice(half * NB, (half + 1) * NB)
                ins = product(acc[half][:], xh[0:n, k, :], xl[0:n, k, :], w0h[0:n, k, cols], w0l[0:n, k, cols],
                              first, end)
                if end:
                    ins.then_inc(s_l[0], 1)

            def upper(layer, half, k):
                wh, wl, dst = (w1h, w1l, acc[half]) if layer == 1 else (w2h, w2l, acc[2])
                cols = slice(half * NB, (half + 1) * NB)
                src, at = k // 4, slice((k % 4) * P, (k % 4 + 1) * P)
                ins = product(dst[:], yh[:, src, at], yl[:, src, at], wh[:, k, cols], wl[:, k, cols],
                              k == 0, k == T0 // P - 1)
                if k == T0 // P - 1:
                    ins.then_inc(s_l[layer], 1)

            def turn(layer, c, half):
                pe.wait_ge(s_e[layer], c + 1 if layer == 2 else 2 * c + half + 1)
                if layer == 0 and half == 0:
                    after(pe, s_y2, c)
                for i in range(NB // P):
                    ins = nc.tensor.transpose(turned[half][:, i * P:(i + 1) * P],
                                              y_evac[:, half, i * P:(i + 1) * P], ident[:])
                ins.then_inc(s_t[layer], 1)

            def split_ready(layer, c, half):
                pe.wait_ge(s_yh[layer], 2 * c + half + 1)
                pe.wait_ge(s_yl[layer], 2 * c + half + 1)

            def layer2(c):
                split_ready(1, c, 0)
                upper(2, 0, 0)
                turn(1, c, 1)
                for k in range(1, 4):
                    upper(2, 0, k)
                split_ready(1, c, 1)
                for k in range(4, 8):
                    upper(2, 0, k)

            def layer3(c):
                pe.wait_ge(s_y2, c + 1)
                after(pe, s_y4, c)
                for o in range(T3 // P):
                    for k in range(T2 // P):
                        ins = nc.tensor.matmul(last[:, o * P:(o + 1) * P], w3[:, k, o * P:(o + 1) * P],
                                               y2T[:, k, :], start=(k == 0), stop=(k == T2 // P - 1))
                ins.then_inc(s_l[3], 1)

            def layer4(c):
                pe.wait_ge(s_y3, c + 1)
                for k in range(T3 // P):
                    ins = nc.tensor.matmul(last[0:1, T3:T3 + P], w4[:, k:k + 1], y3T[:, k, :],
                                           start=(k == 0), stop=(k == T3 // P - 1))
                ins.then_inc(s_l[4], 1)

            pe.wait_ge(s_ident, 1)
            pe.wait_ge(s_dense, 16)
            for c in range(CHUNKS):
                ins = nc.tensor.transpose(turned[1][0:DENSE, c * P:(c + 1) * P], x0[:, c, :], ident[:])
            ins.then_inc(s_x0t, 1)
            pe.wait_ge(s_botw, 6 * 16)
            pe.wait_ge(s_x0, 1)
            for o in range(B0 // P):
                nc.tensor.matmul((acc + [last])[o][:], v0[:, o * P:(o + 1) * P], x0T[:], start=True,
                                 stop=True).then_inc(s_l0b, 1)
            for k in range(B0 // P):
                pe.wait_ge(s_h0, k + 1)
                for o in range(B1 // P):
                    ins = nc.tensor.matmul(turned[o][:], v1[:, k, o * P:(o + 1) * P], h0T[:, k, :],
                                           start=(k == 0), stop=(k == B0 // P - 1))
                    if k == B0 // P - 1:
                        ins.then_inc(s_l1b, 1)
            for k in range(B1 // P):
                pe.wait_ge(s_h1, k + 1)
                ins = nc.tensor.matmul(acc[0][:], v2[:, k, :], h1T[:, k, :], start=(k == 0),
                                       stop=(k == B1 // P - 1))
            ins.then_inc(s_l2b, 1)
            for j in range(LOTS):
                turn_lot(0, j)

            def chunk(c):
                first = isinstance(c, int) and c == 0
                end = isinstance(c, int) and c == CHUNKS - 1
                dots_of(c)
                if first:
                    pe.wait_ge(s_wl, total)
                    pe.wait_ge(s_topw, 6 * 16)
                else:
                    layer2(c - 1)
                pe.wait_ge(s_xhb, c + 1)
                pe.wait_ge(s_xlb, c + 1)
                layer0(c, 0, BOT_TILE, first=True)
                if not first:
                    turn(2, c - 1, 0)
                pe.wait_ge(s_xhp, c + 1)
                pe.wait_ge(s_xlp, c + 1)
                for k in range(PAIR_TILES):
                    layer0(c, 0, k, end=(k == PAIR_TILES - 1))
                if not first:
                    layer3(c - 1)
                layer0(c, 1, BOT_TILE, first=True)
                turn(0, c, 0)
                layer0(c, 1, 0)
                if not first:
                    layer4(c - 1)
                layer0(c, 1, 1)
                layer0(c, 1, 2, end=True)
                split_ready(0, c, 0)
                upper(1, 0, 0)
                turn(0, c, 1)
                steps = [(0, 1), (0, 2), (0, 3), (1, 0), (1, 1), (1, 2), (1, 3), (0, 4), (0, 5), (0, 6), (0, 7)]
                for at, (half, k) in enumerate(steps):
                    if (half, k) == (0, 4):
                        split_ready(0, c, 1)
                    upper(1, half, k)
                    if 2 <= at < 2 + LOTS and not end:
                        turn_lot(c + 1, at - 2)
                upper(1, 1, 4)
                upper(1, 1, 5)
                turn(1, c, 0)
                upper(1, 1, 6)
                upper(1, 1, 7)

            for c in range(CHUNKS):
                chunk(c)
            layer2(CHUNKS - 1)
            turn(2, CHUNKS - 1, 0)
            layer3(CHUNKS - 1)
            layer4(CHUNKS - 1)


_BOT = [("L0_rec_bw%d" % i, "L0_rec_bb%d" % i) for i in range(3)]
_TOP = [("L0_rec_tw%d" % i, "L0_rec_tb%d" % i) for i in range(5)]
_INS = ["r_dense_x", "r_sparse_x", "L0_rec_emb"] + [n for pair in _BOT + _TOP for n in pair]


def kernel(**inputs):
    import concourse.bacc as bacc
    from concourse.bass_utils import run_bass_kernel_spmd as run

    nc = bacc.Bacc("TRN2", target_bir_lowering=False, num_devices=1)
    arrays, aps = {}, {}
    for name in _INS:
        a = np.ascontiguousarray(inputs[name])
        arrays["in_" + name] = a
        aps[name] = nc.dram_tensor("in_" + name, a.shape, mybir.dt.from_np(a.dtype), kind="ExternalInput").ap()
    arrays["pair_rows"] = pair_row_table()
    pair_rows = nc.dram_tensor("pair_rows", (PAIR_ROWS, PAIR_TILES), U32, kind="ExternalInput").ap()
    scratch = nc.dram_tensor("pair_scratch", (FEATS, WRAP, P), F32, kind="Internal").ap()
    out = nc.dram_tensor("out_y", (BATCH, 1), F32, kind="ExternalOutput").ap()
    rec_kernel(nc, aps["r_dense_x"], aps["r_sparse_x"], aps["L0_rec_emb"],
               [aps[w] for w, _ in _BOT], [aps[b] for _, b in _BOT],
               [aps[w] for w, _ in _TOP], [aps[b] for _, b in _TOP], pair_rows, scratch, out)
    result = run(nc, [arrays], core_ids=[0])
    return result.results[0]["out_y"]
```

```python
from contextlib import ExitStack

import numpy as np
import concourse.bass as bass
from concourse import mybir
from concourse.alu_op_type import AluOpType as ALU

F32 = mybir.dt.float32
F32R = mybir.dt.float32r
I32 = mybir.dt.int32
U32 = mybir.dt.uint32
ACT = mybir.ActivationFunctionType

P = 128
BATCH, DENSE = 512, 13
CHUNKS = BATCH // P
TABLES, VOCAB, DIM = 26, 6250, 128
FEATS = TABLES + 1
SLOT = 32
LOT = 4
LOTS = -(-TABLES // LOT)
ACT_LOTS = (LOTS + 1) // 2
DVE_LOTS = LOTS // 2
GROUP = 4
BANK_GROUPS = 4
Z_BANKS = P // (GROUP * BANK_GROUPS)
HOPS = (FEATS - 1) // 2
PAIR_TILES = 3
PAIR_ROWS = FEATS * HOPS // PAIR_TILES
WRAP = FEATS + HOPS
BOT_TILE = PAIR_TILES
B0, B1, B2 = 512, 256, 128
T0, T1, T2, T3 = 1024, 1024, 512, 256
NB = 512
STAGES = 3


def pair_row_table():
    table = np.zeros((PAIR_ROWS, PAIR_TILES), np.uint32)
    for i in range(PAIR_TILES):
        for p in range(PAIR_ROWS):
            n = i * (FEATS // PAIR_TILES) + p // HOPS
            m = (n + p % HOPS + 1) % FEATS
            a, b = max(n, m), min(n, m)
            table[p, i] = DIM + a * (a - 1) // 2 + b
    return table


def flat(ap, offset, dims):
    return bass.AP(tensor=ap.tensor, offset=offset, ap=dims)


def after(eng, sem, count):
    if not isinstance(count, int) or count > 0:
        eng.wait_ge(sem, count)


def rec_kernel(nc, dense, sparse, emb, bw, bb, tw, tb, pair_rows, scratch, out):
    with ExitStack() as ctx:
        def sb(name, shape, dt=F32, scope=ctx):
            return scope.enter_context(nc.sbuf_tensor(name, shape, dt))

        def sem(name):
            return ctx.enter_context(nc.semaphore(name))

        w0h = sb("w0h", [P, PAIR_TILES + 1, T0], F32R)
        w0l = sb("w0l", [P, PAIR_TILES + 1, T0], F32R)
        w1h = sb("w1h", [P, T0 // P, T1], F32R)
        w1l = sb("w1l", [P, T0 // P, T1], F32R)
        w2h = sb("w2h", [P, T1 // P, T2], F32R)
        w2l = sb("w2l", [P, T1 // P, T2], F32R)
        w3 = sb("w3", [P, T2 // P, T3])
        w4 = sb("w4", [P, T3 // P])
        bias1 = sb("bias1", [P, T1])
        bias2 = sb("bias2", [P, T2])
        bias3 = sb("bias3", [P, T3 // P])
        bias4 = sb("bias4", [1, 1])
        ident = sb("ident", [P, P])
        botT = sb("botT", [P, BATCH])
        rows = sb("rows", [P, TABLES, DIM])
        featT = sb("featT", [P, P, SLOT])
        pairs = sb("pairs", [P, PAIR_TILES, P])
        index_raw = sb("index_raw", [P, CHUNKS, TABLES], I32)
        index_tmp = sb("index_tmp", [P, CHUNKS, TABLES])
        index_base = sb("index_base", [P, CHUNKS, TABLES], I32)
        index = sb("index", [P, CHUNKS, TABLES], U32)
        pair_index = sb("pair_index", [PAIR_ROWS, PAIR_TILES], U32)

        with ExitStack() as early:
            x0 = sb("x0", [P, CHUNKS, DENSE], F32, early)
            x0T = sb("x0T", [DENSE, BATCH], F32, early)
            v0 = sb("v0", [DENSE, B0], F32, early)
            v1 = sb("v1", [P, B0 // P, B1], F32, early)
            v2 = sb("v2", [P, B1 // P, B2], F32, early)
            c0 = sb("c0", [P, B0 // P], F32, early)
            c1 = sb("c1", [P, B1 // P], F32, early)
            c2 = sb("c2", [P, 1], F32, early)
            h0T = sb("h0T", [P, B0 // P, BATCH], F32, early)
            h1T = sb("h1T", [P, B1 // P, BATCH], F32, early)
        dots = sb("dots", [FEATS, FEATS, P])
        y_evac = sb("y_evac", [P, 2, NB])
        y2T = sb("y2T", [P, T2 // P, P])
        y3T = sb("y3T", [P, T3 // P, P])
        out_row = sb("out_row", [1, BATCH])
        with ExitStack() as early:
            stage = sb("stage", [P, STAGES, 1024], F32, early)
        xh = sb("xh", [P, PAIR_TILES + 1, P], F32R)
        xl = sb("xl", [P, PAIR_TILES + 1, P], F32R)
        yh = sb("yh", [P, 2, NB], F32R)
        yl = sb("yl", [P, 2, NB], F32R)

        def bank(name):
            return ctx.enter_context(nc.psum_tensor(name, [P, NB], F32))

        acc = [bank("acc0"), bank("acc1"), bank("acc2")]
        turned = [bank("turned0"), bank("turned1")]
        fz = [bank("fz0"), bank("fz1")]
        last = bank("last")

        s_sparse, s_dense, s_pidx, s_botb, s_topw, s_one = map(
            sem, ("sparse_in", "dense_in", "pair_index_in", "bottom_biases_in", "top_small_in", "ones_set"))
        s_v = [sem(f"bottom_weights{i}_in") for i in range(3)]
        s_base, s_ident0, s_ident, s_chain, s_index, s_pad = map(
            sem, ("index_base_set", "ident_zero", "ident_set", "index_chain", "index_ready", "pad_set"))
        s_stage = [sem(f"staged{i}") for i in range(STAGES)]
        s_pair = [sem(f"pair_weights_in{i}") for i in range(PAIR_TILES)]
        s_brow = sem("bias_row_in")
        s_wh, s_wl = sem("weight_hi"), sem("weight_lo")
        s_x0t, s_x0, s_l0b, s_h0, s_l1b, s_h1, s_l2b, s_bot = map(
            sem, ("x0_turned", "x0T_ready", "bot0_done", "h0_ready", "bot1_done", "h1_ready", "bot2_done",
                  "botT_ready"))
        s_gather = [sem(f"gathered{j}") for j in range(LOTS)]
        s_ft, s_fa, s_fd, s_fb = map(sem, ("lot_turned", "lot_copied_act", "lot_copied_dve", "bot_feature_copied"))
        s_z, s_za, s_zd = map(sem, ("dots_done", "dots_copied_act", "dots_copied_dve"))
        s_scr, s_pin = sem("scratch_written"), sem("pairs_in")
        s_xhb, s_xlb, s_xhp, s_xlp = map(sem, ("bot_hi", "bot_lo", "pairs_hi", "pairs_lo"))
        s_l = [sem(f"layer{i}_done") for i in range(5)]
        s_e = [sem(f"layer{i}_copied") for i in range(3)]
        s_t = [sem(f"layer{i}_turned") for i in range(3)]
        s_yh = [sem(f"layer{i}_hi") for i in range(2)]
        s_yl = [sem(f"layer{i}_lo") for i in range(2)]
        s_y2, s_y3, s_y4, s_out = map(sem, ("y2T_ready", "y3T_ready", "out_ready", "out_written"))

        def pair_piece(i):
            k = PAIR_ROWS + (i == PAIR_TILES - 1)
            return w0h[0:k, i, :], w0l[0:k, i, :], k

        pieces = [(w0h[:, BOT_TILE, :], w0l[:, BOT_TILE, :], P)]
        sources = [tw[0][0:P, :]]
        for k in range(T0 // P):
            pieces.append((w1h[:, k, :], w1l[:, k, :], P))
            sources.append(tw[1][k * P:(k + 1) * P, :])
        for k in range(0, T1 // P, 2):
            pieces.append((w2h[:, k:k + 2, :].rearrange("p k n -> p (k n)"),
                           w2l[:, k:k + 2, :].rearrange("p k n -> p (k n)"), P))
            sources.append(tw[2][k * P:(k + 2) * P, :].rearrange("(k p) n -> p k n", p=P))
        direct = len(pieces)
        pieces += [pair_piece(i) for i in range(PAIR_TILES)]
        total = len(pieces)

        def piece_in(eng, n):
            if n < direct:
                eng.wait_ge(s_stage[n % STAGES], 16 * (n // STAGES + 1))
            else:
                eng.wait_ge(s_pair[n - direct], 16)
            if n == total - 1:
                eng.wait_ge(s_brow, 16)

        def dot_quadrant(z, s):
            at = z * GROUP * BANK_GROUPS + s
            to = dots[:, :, at:at + GROUP * (BANK_GROUPS - 1) + 1:GROUP].rearrange("n m g -> n g m")
            block_ = fz[z % 2][SLOT * s:SLOT * s + FEATS, 0:BANK_GROUPS * GROUP * FEATS]
            return to, block_.rearrange("n (g c) -> n g c", g=BANK_GROUPS)[:, :, s * FEATS:(s + 1) * FEATS]

        block = ctx.enter_context(nc.Block())

        @block.sync
        def _(sp):
            sp.dma_start(index_raw[:], sparse.rearrange("(c p) t -> p c t", p=P)).then_inc(s_sparse, 16)
            sp.dma_start(x0[:], dense.rearrange("(c p) d -> p c d", p=P)).then_inc(s_dense, 16)
            sp.dma_start(v0[:], bw[0]).then_inc(s_v[0], 16)

            def load_piece(n):
                after(sp, s_wl, n - STAGES + 1)
                dst = stage[:, n % STAGES, :]
                if len(sources[n].shape) == 3:
                    dst = dst.rearrange("p (k n) -> p k n", k=2)
                sp.dma_start(dst, sources[n]).then_inc(s_stage[n % STAGES], 16)

            load_piece(0)
            sp.dma_start(v1[:], bw[1].rearrange("(k p) n -> p k n", p=P)).then_inc(s_v[1], 16)
            load_piece(1)
            sp.dma_start(v2[:], bw[2].rearrange("(k p) n -> p k n", p=P)).then_inc(s_v[2], 16)
            load_piece(2)
            for n in range(STAGES, direct):
                load_piece(n)
            sp.wait_ge(s_wl, total - STAGES)
            sp.dma_start(stage[PAIR_ROWS:PAIR_ROWS + 1, (total - 1) % STAGES, :],
                         tb[0].rearrange("(o n) -> o n", o=1)).then_inc(s_brow, 16)
            sp.dma_start(w3[:], tw[3].rearrange("(k p) n -> p k n", p=P)).then_inc(s_topw, 16)
            sp.dma_start(w4[:], tw[4].rearrange("(k p) n -> p (k n)", p=P), allow_slow_non_contiguous=True).then_inc(s_topw, 16)
            sp.dma_start(bias1[:], flat(tb[1], 0, [[0, P], [1, T1]])).then_inc(s_topw, 16)
            sp.dma_start(bias2[:], flat(tb[2], 0, [[0, P], [1, T2]])).then_inc(s_topw, 16)

            def regroup(c):
                sp.wait_ge(s_za, Z_BANKS * (c + 1))
                sp.wait_ge(s_zd, Z_BANKS * (c + 1))
                after(sp, s_pin, 16 * PAIR_TILES * c)
                sp.dma_start(scratch[:, 0:FEATS, :], dots[:]).then_inc(s_scr, 16)
                sp.dma_start(scratch[:, FEATS:WRAP, :], dots[:, 0:HOPS, :]).then_inc(s_scr, 16)
                sp.wait_ge(s_scr, 32 * (c + 1))
                after(sp, s_xlp, c)
                if isinstance(c, int) and c == 0:
                    sp.wait_ge(s_one, 1)
                for i in range(PAIR_TILES):
                    tile_feats = FEATS // PAIR_TILES
                    src = flat(scratch, (i * tile_feats * (WRAP + 1) + 1) * P,
                               [[(WRAP + 1) * P, tile_feats], [P, HOPS], [1, P]])
                    sp.dma_start(pairs[0:PAIR_ROWS, i, :], src).then_inc(s_pin, 16)

            for c in range(CHUNKS):
                regroup(c)
            sp.wait_ge(s_y4, CHUNKS)
            sp.dma_start(out.rearrange("b o -> o b"), out_row[:]).then_inc(s_out, 16)
            sp.wait_ge(s_out, 16)

        @block.gpsimd
        def _(pool):
            pool.iota(index_base[:], pattern=[[0, CHUNKS], [VOCAB, TABLES]], base=0,
                      channel_multiplier=0).then_inc(s_base, 1)
            pool.memset(ident[:], 0.0).then_inc(s_ident0, 1)
            pool.wait_ge(s_ident0, 1)
            pool.affine_select(out=ident[:], in_=ident[:], compare_op=ALU.not_equal, fill=1.0, base=0,
                               pattern=[[-1, P]], channel_multiplier=1).then_inc(s_ident, 1)
            table = emb.rearrange("t v d -> (t v) d")

            def gather_chunk(c):
                for t in range(TABLES):
                    if t % LOT == 0:
                        after(pool, s_ft, LOTS * (c - 1) + t // LOT + 1)
                    pool.indirect_dma_start(
                        rows[:, t, :], None, table,
                        bass.IndirectOffsetOnAxis(ap=index[:, c, t:t + 1], axis=0)).then_inc(s_gather[t // LOT], 16)

            pool.wait_ge(s_index, 1)
            gather_chunk(0)
            pool.wait_ge(s_pidx, 16)
            for i in range(PAIR_TILES):
                n = direct + i
                pool.wait_ge(s_wl, n - STAGES + 1)
                pool.indirect_dma_start(
                    stage[0:PAIR_ROWS, n % STAGES, :], None, tw[0],
                    bass.IndirectOffsetOnAxis(ap=pair_index[:, i:i + 1], axis=0)).then_inc(s_pair[i], 16)
            for c in range(1, CHUNKS):
                gather_chunk(c)

        @block.scalar
        def _(act):
            act.dma_start(c0[:], bb[0].rearrange("(k p) -> p k", p=P), allow_slow_non_contiguous=True).then_inc(s_botb, 16)
            act.dma_start(c1[:], bb[1].rearrange("(k p) -> p k", p=P), allow_slow_non_contiguous=True).then_inc(s_botb, 16)
            act.dma_start(c2[:], bb[2].rearrange("(k p) -> p k", p=P), allow_slow_non_contiguous=True).then_inc(s_botb, 16)
            act.dma_start(pair_index[:], pair_rows).then_inc(s_pidx, 16)
            act.dma_start(bias3[:], tb[3].rearrange("(k p) -> p k", p=P), allow_slow_non_contiguous=True).then_inc(s_topw, 16)
            act.dma_start(bias4[:], tb[4].rearrange("(o n) -> o n", o=1)).then_inc(s_topw, 16)

            def weight_hi(n):
                hi, _, k = pieces[n]
                piece_in(act, n)
                nc.scalar.copy(hi, stage[0:k, n % STAGES, :]).then_inc(s_wh, 1)

            def feature_lot(c, j):
                act.wait_ge(s_ft, LOTS * c + j + 1)
                w = min(LOT, TABLES - LOT * j)
                nc.scalar.copy(
                    featT[:, :, 1 + LOT * j:1 + LOT * j + w].rearrange("d b n -> d n b"),
                    fz[j % 2][:, 0:w * P].rearrange("d (n b) -> d n b", b=P)).then_inc(s_fa, 1)

            def dots_out(c, between):
                after(act, s_scr, 32 * c)
                for z in range(Z_BANKS):
                    if z in between:
                        weight_hi(between[z])
                    act.wait_ge(s_z, Z_BANKS * c + z + 1)
                    for s in (0, 1):
                        ins = nc.scalar.copy(*dot_quadrant(z, s))
                    ins.then_inc(s_za, 1)

            def split_hi(layer, c, half):
                act.wait_ge(s_t[layer], 2 * c + half + 1)
                nc.scalar.activation(yh[:, half, :], turned[half][:], ACT.Relu).then_inc(s_yh[layer], 1)

            def bot_hi(c):
                after(act, s_l[0], 2 * c)
                nc.scalar.copy(xh[:, BOT_TILE, :], botT[:, c * P:(c + 1) * P]).then_inc(s_xhb, 1)

            def pairs_hi(c):
                act.wait_ge(s_pin, 16 * PAIR_TILES * (c + 1))
                after(act, s_l[0], 2 * c)
                nc.scalar.copy(xh[0:PAIR_ROWS + 1, 0:PAIR_TILES, :],
                               pairs[0:PAIR_ROWS + 1, :, :]).then_inc(s_xhp, 1)

            def layer2_out(c):
                act.wait_ge(s_t[2], c + 1)
                nc.scalar.activation(y2T[:].rearrange("p k b -> p (k b)"), turned[0][:],
                                     ACT.Relu).then_inc(s_y2, 1)

            def layer3_out(c):
                act.wait_ge(s_l[3], c + 1)
                for o in range(T3 // P):
                    ins = nc.scalar.activation(y3T[:, o, :], last[:, o * P:(o + 1) * P], ACT.Relu,
                                               bias=bias3[:, o:o + 1])
                ins.then_inc(s_y3, 1)

            def layer4_out(c):
                act.wait_ge(s_l[4], c + 1)
                nc.scalar.activation(out_row[0:1, c * P:(c + 1) * P], last[0:1, T3:T3 + P], ACT.Relu,
                                     bias=bias4[:]).then_inc(s_y4, 1)

            def bottom0(o):
                act.wait_ge(s_l0b, o + 1)
                nc.scalar.activation(h0T[:, o, :], (acc + [last])[o][:], ACT.Relu,
                                     bias=c0[:, o:o + 1]).then_inc(s_h0, 1)

            def bottom1(o):
                act.wait_ge(s_l1b, o + 1)
                nc.scalar.activation(h1T[:, o, :], turned[o][:], ACT.Relu, bias=c1[:, o:o + 1]).then_inc(s_h1, 1)

            def bottom2():
                act.wait_ge(s_l2b, 1)
                nc.scalar.activation(botT[:], acc[0][:], ACT.Relu, bias=c2[:]).then_inc(s_bot, 1)

            act.wait_ge(s_botb, 3 * 16)
            act.wait_ge(s_pad, 1)
            weight_hi(0)
            bottom0(0)
            bottom0(1)
            weight_hi(1)
            bottom0(2)
            weight_hi(2)
            bottom0(3)
            feature_lot(0, 0)
            for n in (3, 4, 5):
                weight_hi(n)
            bottom1(0)
            weight_hi(6)
            bottom1(1)
            feature_lot(0, 2)
            weight_hi(7)
            bottom2()
            for n in (8, 9):
                weight_hi(n)
            feature_lot(0, 4)
            for n in (10, 11):
                weight_hi(n)
            feature_lot(0, 6)
            weight_hi(12)
            def chunk(c):
                first = isinstance(c, int) and c == 0
                end = isinstance(c, int) and c == CHUNKS - 1
                if not first:
                    bot_hi(c)
                dots_out(c, {3: direct, 5: direct + 1, 7: direct + 2} if first else {})
                if first:
                    act.wait_ge(s_wl, total)
                    bot_hi(c)
                else:
                    split_hi(1, c - 1, 1)
                    layer2_out(c - 1)
                if not end:
                    feature_lot(c + 1, 0)
                pairs_hi(c)
                if not first:
                    layer3_out(c - 1)
                    layer4_out(c - 1)
                if not end:
                    feature_lot(c + 1, 2)
                split_hi(0, c, 0)
                split_hi(0, c, 1)
                if not end:
                    for j in range(4, LOTS, 2):
                        feature_lot(c + 1, j)
                split_hi(1, c, 0)

            for c in range(CHUNKS):
                chunk(c)
            split_hi(1, CHUNKS - 1, 1)
            layer2_out(CHUNKS - 1)
            layer3_out(CHUNKS - 1)
            layer4_out(CHUNKS - 1)

        @block.vector
        def _(dve):
            nc.vector.memset(featT[:, :, FEATS:SLOT], 0.0).then_inc(s_pad, 1)
            nc.vector.memset(pairs[96:P, :, :], 1.0).then_inc(s_one, 1)
            dve.wait_ge(s_sparse, 16)
            nc.vector.tensor_scalar(index_tmp[:], index_raw[:], 0.0, float(VOCAB), ALU.is_lt,
                                    ALU.mult).then_inc(s_chain, 1)
            dve.wait_ge(s_chain, 1)
            nc.vector.tensor_tensor(index_tmp[:], index_tmp[:], index_raw[:], ALU.add).then_inc(s_chain, 1)
            dve.wait_ge(s_chain, 2)
            nc.vector.tensor_scalar(index_tmp[:], index_tmp[:], 0.0, float(VOCAB - 1), ALU.max,
                                    ALU.min).then_inc(s_chain, 1)
            dve.wait_ge(s_chain, 3)
            dve.wait_ge(s_base, 1)
            nc.vector.tensor_tensor(index[:], index_tmp[:], index_base[:], ALU.add).then_inc(s_index, 1)

            def weight_lo(n):
                hi, lo, k = pieces[n]
                dve.wait_ge(s_wh, n + 1)
                nc.vector.tensor_tensor(lo, stage[0:k, n % STAGES, :], hi.bitcast(F32),
                                        ALU.subtract).then_inc(s_wl, 1)

            def feature_lot(c, j):
                dve.wait_ge(s_ft, LOTS * c + j + 1)
                nc.vector.tensor_copy(
                    featT[:, :, 1 + LOT * j:1 + LOT * (j + 1)].rearrange("d b n -> d n b"),
                    fz[j % 2][:].rearrange("d (n b) -> d n b", b=P)).then_inc(s_fd, 1)

            def bot_feature(c):
                dve.wait_ge(s_ft, LOTS * c + 1)
                nc.vector.tensor_copy(featT[:, :, 0], botT[:, c * P:(c + 1) * P]).then_inc(s_fb, 1)

            def dots_out(c, between):
                after(dve, s_scr, 32 * c)
                for z in range(Z_BANKS):
                    if z in between:
                        weight_lo(between[z])
                    dve.wait_ge(s_z, Z_BANKS * c + z + 1)
                    for s in (2, 3):
                        ins = nc.vector.tensor_copy(*dot_quadrant(z, s))
                    ins.then_inc(s_zd, 1)

            def bot_lo(c):
                dve.wait_ge(s_xhb, c + 1)
                nc.vector.tensor_tensor(xl[:, BOT_TILE, :], botT[:, c * P:(c + 1) * P],
                                        xh[:, BOT_TILE, :].bitcast(F32), ALU.subtract).then_inc(s_xlb, 1)

            def pairs_lo(c):
                dve.wait_ge(s_xhp, c + 1)
                nc.vector.tensor_tensor(xl[0:PAIR_ROWS + 1, 0:PAIR_TILES, :], pairs[0:PAIR_ROWS + 1, :, :],
                                        xh[0:PAIR_ROWS + 1, 0:PAIR_TILES, :].bitcast(F32),
                                        ALU.subtract).then_inc(s_xlp, 1)

            def copy_out(layer, c, half):
                if layer == 2:
                    dve.wait_ge(s_l[2], c + 1)
                    nc.vector.tensor_tensor(y_evac[:, 0, :], acc[2][:], bias2[:], ALU.add).then_inc(s_e[2], 1)
                    return
                dve.wait_ge(s_l[layer], 2 * c + half + 1)
                if layer == 0:
                    ins = nc.vector.tensor_copy(y_evac[:, half, :], acc[half][:])
                else:
                    ins = nc.vector.tensor_tensor(y_evac[:, half, :], acc[half][:],
                                                  bias1[:, half * NB:(half + 1) * NB], ALU.add)
                ins.then_inc(s_e[layer], 1)

            def split_lo(layer, c, half):
                dve.wait_ge(s_yh[layer], 2 * c + half + 1)
                nc.vector.scalar_tensor_tensor(out=yl[:, half, :], in0=turned[half][:], scalar=0.0,
                                               in1=yh[:, half, :].bitcast(F32), op0=ALU.max,
                                               op1=ALU.subtract).then_inc(s_yl[layer], 1)

            dve.wait_ge(s_x0t, 1)
            nc.vector.tensor_copy(x0T[:], turned[1][0:DENSE, :]).then_inc(s_x0, 1)
            for n in range(5):
                weight_lo(n)
            feature_lot(0, 1)
            for n in range(5, 8):
                weight_lo(n)
            feature_lot(0, 3)
            dve.wait_ge(s_bot, 1)
            bot_feature(0)
            for n in range(8, direct - 1):
                weight_lo(n)
            feature_lot(0, 5)
            weight_lo(direct - 1)

            def chunk(c):
                first = isinstance(c, int) and c == 0
                end = isinstance(c, int) and c == CHUNKS - 1
                if not first:
                    bot_lo(c)
                dots_out(c, {3: direct, 5: direct + 1, 7: direct + 2} if first else {})
                if first:
                    bot_lo(c)
                else:
                    split_lo(1, c - 1, 1)
                    copy_out(2, c - 1, 0)
                pairs_lo(c)
                if not end:
                    feature_lot(c + 1, 1)
                copy_out(0, c, 0)
                split_lo(0, c, 0)
                copy_out(0, c, 1)
                if not end:
                    feature_lot(c + 1, 3)
                split_lo(0, c, 1)
                if not end:
                    for j in range(5, LOTS, 2):
                        feature_lot(c + 1, j)
                    bot_feature(c + 1)
                copy_out(1, c, 0)
                split_lo(1, c, 0)
                copy_out(1, c, 1)

            for c in range(CHUNKS):
                chunk(c)
            split_lo(1, CHUNKS - 1, 1)
            copy_out(2, CHUNKS - 1, 0)

        @block.tensor
        def _(pe):
            def turn_lot(c, j):
                w = min(LOT, TABLES - LOT * j)
                pe.wait_ge(s_gather[j], 16 * w * (c + 1))
                if j < 2:
                    after(pe, s_za, Z_BANKS * c)
                    after(pe, s_zd, Z_BANKS * c)
                elif j % 2 == 0:
                    pe.wait_ge(s_fa, ACT_LOTS * c + j // 2)
                else:
                    pe.wait_ge(s_fd, DVE_LOTS * c + j // 2)
                for i in range(w):
                    ins = nc.tensor.transpose(fz[j % 2][:, i * P:(i + 1) * P], rows[:, LOT * j + i, :], ident[:])
                ins.then_inc(s_ft, 1)

            def dots_of(c):
                pe.wait_ge(s_fa, ACT_LOTS * (c + 1))
                pe.wait_ge(s_fd, DVE_LOTS * (c + 1))
                pe.wait_ge(s_fb, c + 1)
                for z in range(Z_BANKS):
                    if z >= 2:
                        pe.wait_ge(s_za, Z_BANKS * c + z - 1)
                        pe.wait_ge(s_zd, Z_BANKS * c + z - 1)
                    for g in range(BANK_GROUPS):
                        b = (z * BANK_GROUPS + g) * GROUP
                        w = GROUP * FEATS
                        w_rows = (GROUP - 1) * SLOT + FEATS
                        ins = nc.tensor.matmul(
                            fz[z % 2][0:w_rows, g * w:(g + 1) * w].rearrange("n (s m) -> n s m", s=GROUP),
                            featT[:, b:b + GROUP, :].rearrange("d s n -> d (s n)")[:, 0:w_rows],
                            featT[:, b:b + GROUP, 0:FEATS], start=True, stop=True)
                    ins.then_inc(s_z, 1)

            def product(dst, ah, al, wh, wl, first, end):
                nc.tensor.matmul(dst, ah, wh, start=first, stop=False)
                nc.tensor.matmul(dst, ah, wl, start=False, stop=False)
                return nc.tensor.matmul(dst, al, wh, start=False, stop=end)

            def layer0(c, half, k, first=False, end=False):
                n = P if k == BOT_TILE else PAIR_ROWS + (k == PAIR_TILES - 1)
                cols = slice(half * NB, (half + 1) * NB)
                ins = product(acc[half][:], xh[0:n, k, :], xl[0:n, k, :], w0h[0:n, k, cols], w0l[0:n, k, cols],
                              first, end)
                if end:
                    ins.then_inc(s_l[0], 1)

            def upper(layer, half, k):
                wh, wl, dst = (w1h, w1l, acc[half]) if layer == 1 else (w2h, w2l, acc[2])
                cols = slice(half * NB, (half + 1) * NB)
                src, at = k // 4, slice((k % 4) * P, (k % 4 + 1) * P)
                ins = product(dst[:], yh[:, src, at], yl[:, src, at], wh[:, k, cols], wl[:, k, cols],
                              k == 0, k == T0 // P - 1)
                if k == T0 // P - 1:
                    ins.then_inc(s_l[layer], 1)

            def turn(layer, c, half):
                pe.wait_ge(s_e[layer], c + 1 if layer == 2 else 2 * c + half + 1)
                if layer == 0 and half == 0:
                    after(pe, s_y2, c)
                for i in range(NB // P):
                    ins = nc.tensor.transpose(turned[half][:, i * P:(i + 1) * P],
                                              y_evac[:, half, i * P:(i + 1) * P], ident[:])
                ins.then_inc(s_t[layer], 1)

            def split_ready(layer, c, half):
                pe.wait_ge(s_yh[layer], 2 * c + half + 1)
                pe.wait_ge(s_yl[layer], 2 * c + half + 1)

            def layer2(c):
                split_ready(1, c, 0)
                upper(2, 0, 0)
                turn(1, c, 1)
                for k in range(1, 4):
                    upper(2, 0, k)
                split_ready(1, c, 1)
                for k in range(4, 8):
                    upper(2, 0, k)

            def layer3(c):
                pe.wait_ge(s_y2, c + 1)
                after(pe, s_y4, c)
                for o in range(T3 // P):
                    for k in range(T2 // P):
                        ins = nc.tensor.matmul(last[:, o * P:(o + 1) * P], w3[:, k, o * P:(o + 1) * P],
                                               y2T[:, k, :], start=(k == 0), stop=(k == T2 // P - 1))
                ins.then_inc(s_l[3], 1)

            def layer4(c):
                pe.wait_ge(s_y3, c + 1)
                for k in range(T3 // P):
                    ins = nc.tensor.matmul(last[0:1, T3:T3 + P], w4[:, k:k + 1], y3T[:, k, :],
                                           start=(k == 0), stop=(k == T3 // P - 1))
                ins.then_inc(s_l[4], 1)

            pe.wait_ge(s_ident, 1)
            pe.wait_ge(s_dense, 16)
            for c in range(CHUNKS):
                ins = nc.tensor.transpose(turned[1][0:DENSE, c * P:(c + 1) * P], x0[:, c, :], ident[:])
            ins.then_inc(s_x0t, 1)
            pe.wait_ge(s_v[0], 16)
            pe.wait_ge(s_x0, 1)
            for o in range(B0 // P):
                nc.tensor.matmul((acc + [last])[o][:], v0[:, o * P:(o + 1) * P], x0T[:], start=True,
                                 stop=True).then_inc(s_l0b, 1)
            turn_lot(0, 0)
            pe.wait_ge(s_v[1], 16)
            for k in range(B0 // P):
                if k == 2:
                    turn_lot(0, 1)
                pe.wait_ge(s_h0, k + 1)
                for o in range(B1 // P):
                    ins = nc.tensor.matmul(turned[o][:], v1[:, k, o * P:(o + 1) * P], h0T[:, k, :],
                                           start=(k == 0), stop=(k == B0 // P - 1))
                    if k == B0 // P - 1:
                        ins.then_inc(s_l1b, 1)
            turn_lot(0, 2)
            pe.wait_ge(s_v[2], 16)
            for k in range(B1 // P):
                pe.wait_ge(s_h1, k + 1)
                ins = nc.tensor.matmul(acc[0][:], v2[:, k, :], h1T[:, k, :], start=(k == 0),
                                       stop=(k == B1 // P - 1))
            ins.then_inc(s_l2b, 1)
            for j in range(3, LOTS):
                turn_lot(0, j)

            def chunk(c):
                first = isinstance(c, int) and c == 0
                end = isinstance(c, int) and c == CHUNKS - 1
                dots_of(c)
                if first:
                    pe.wait_ge(s_wl, 1)
                else:
                    layer2(c - 1)
                pe.wait_ge(s_xhb, c + 1)
                pe.wait_ge(s_xlb, c + 1)
                layer0(c, 0, BOT_TILE, first=True)
                layer0(c, 1, BOT_TILE, first=True)
                if not first:
                    turn(2, c - 1, 0)
                if not end:
                    turn_lot(c + 1, 0)
                if not first:
                    layer3(c - 1)
                if not end:
                    turn_lot(c + 1, 1)
                if first:
                    pe.wait_ge(s_wl, total)
                pe.wait_ge(s_xhp, c + 1)
                pe.wait_ge(s_xlp, c + 1)
                layer0(c, 0, 0)
                if not first:
                    layer4(c - 1)
                layer0(c, 0, 1)
                layer0(c, 0, 2, end=True)
                layer0(c, 1, 0)
                if not end:
                    turn_lot(c + 1, 2)
                turn(0, c, 0)
                layer0(c, 1, 1)
                layer0(c, 1, 2, end=True)
                if not end:
                    turn_lot(c + 1, 3)
                if first:
                    pe.wait_ge(s_topw, 6 * 16)
                split_ready(0, c, 0)
                upper(1, 0, 0)
                turn(0, c, 1)
                steps = [(0, 1), (0, 2), (0, 3), (1, 0), (1, 1), (1, 2), (1, 3), (0, 4), (0, 5), (0, 6), (0, 7)]
                for at, (half, k) in enumerate(steps):
                    if (half, k) == (0, 4):
                        split_ready(0, c, 1)
                    upper(1, half, k)
                    if 4 <= at < LOTS and not end:
                        turn_lot(c + 1, at)
                upper(1, 1, 4)
                upper(1, 1, 5)
                turn(1, c, 0)
                upper(1, 1, 6)
                upper(1, 1, 7)

            for c in range(CHUNKS):
                chunk(c)
            layer2(CHUNKS - 1)
            turn(2, CHUNKS - 1, 0)
            layer3(CHUNKS - 1)
            layer4(CHUNKS - 1)


_BOT = [("L0_rec_bw%d" % i, "L0_rec_bb%d" % i) for i in range(3)]
_TOP = [("L0_rec_tw%d" % i, "L0_rec_tb%d" % i) for i in range(5)]
_INS = ["r_dense_x", "r_sparse_x", "L0_rec_emb"] + [n for pair in _BOT + _TOP for n in pair]


def kernel(**inputs):
    import concourse.bacc as bacc
    from concourse.bass_utils import run_bass_kernel_spmd as run

    nc = bacc.Bacc("TRN2", target_bir_lowering=False, num_devices=1)
    arrays, aps = {}, {}
    for name in _INS:
        a = np.ascontiguousarray(inputs[name])
        arrays["in_" + name] = a
        aps[name] = nc.dram_tensor("in_" + name, a.shape, mybir.dt.from_np(a.dtype), kind="ExternalInput").ap()
    arrays["pair_rows"] = pair_row_table()
    pair_rows = nc.dram_tensor("pair_rows", (PAIR_ROWS, PAIR_TILES), U32, kind="ExternalInput").ap()
    scratch = nc.dram_tensor("pair_scratch", (FEATS, WRAP, P), F32, kind="Internal").ap()
    out = nc.dram_tensor("out_y", (BATCH, 1), F32, kind="ExternalOutput").ap()
    rec_kernel(nc, aps["r_dense_x"], aps["r_sparse_x"], aps["L0_rec_emb"],
               [aps[w] for w, _ in _BOT], [aps[b] for _, b in _BOT],
               [aps[w] for w, _ in _TOP], [aps[b] for _, b in _TOP], pair_rows, scratch, out)
    result = run(nc, [arrays], core_ids=[0])
    return result.results[0]["out_y"]
```

```python
from contextlib import ExitStack

import numpy as np
import concourse.bass as bass
from concourse import mybir
from concourse.alu_op_type import AluOpType as ALU

F32 = mybir.dt.float32
F32R = mybir.dt.float32r
I32 = mybir.dt.int32
U32 = mybir.dt.uint32
ACT = mybir.ActivationFunctionType

P = 128
BATCH, DENSE = 512, 13
CHUNKS = BATCH // P
TABLES, VOCAB, DIM = 26, 6250, 128
FEATS = TABLES + 1
SLOT = 32
LOT = 4
LOTS = -(-TABLES // LOT)
ACT_LOTS = (LOTS + 1) // 2
DVE_LOTS = LOTS // 2
GROUP = 4
BANK_GROUPS = 4
Z_BANKS = P // (GROUP * BANK_GROUPS)
HOPS = (FEATS - 1) // 2
PAIR_TILES = 3
TILE_FEATS = FEATS // PAIR_TILES
PAIR_ROWS = TILE_FEATS * HOPS
WRAP = FEATS + HOPS
B0, B1, B2 = 512, 256, 128
T0, T1, T2, T3 = 1024, 1024, 512, 256
NB = 512
STAGES = 3


def pair_row_table():
    table = np.zeros((PAIR_ROWS, PAIR_TILES), np.uint32)
    for i in range(PAIR_TILES):
        for p in range(PAIR_ROWS):
            n = i * TILE_FEATS + p // HOPS
            m = (n + p % HOPS + 1) % FEATS
            a, b = max(n, m), min(n, m)
            table[p, i] = DIM + a * (a - 1) // 2 + b
    return table


def flat(ap, offset, dims):
    return bass.AP(tensor=ap.tensor, offset=offset, ap=dims)


def after(eng, sem, count):
    if count > 0:
        eng.wait_ge(sem, count)


def rec_kernel(nc, dense, sparse, emb, bw, bb, tw, tb, pair_rows, scratch, out):
    with ExitStack() as ctx:
        def sb(name, shape, dt=F32, scope=ctx):
            return scope.enter_context(nc.sbuf_tensor(name, shape, dt))

        def sem(name):
            return ctx.enter_context(nc.semaphore(name))

        w0h = sb("w0h", [P, PAIR_TILES, T0], F32R)
        w0l = sb("w0l", [P, PAIR_TILES, T0], F32R)
        w1h = sb("w1h", [P, T0 // P, T1], F32R)
        w1l = sb("w1l", [P, T0 // P, T1], F32R)
        w2h = sb("w2h", [P, T1 // P, T2], F32R)
        w2l = sb("w2l", [P, T1 // P, T2], F32R)
        BOT_W, BOT_X = slice(4, 6), 6
        bot_part = sb("bot_part", [P, CHUNKS - 1, T0])
        w3 = sb("w3", [P, T2 // P, T3])
        w4 = sb("w4", [P, T3 // P])
        bias3 = sb("bias3", [P, T3 // P])
        bias4 = sb("bias4", [1, 1])
        ident = sb("ident", [P, P])
        botT = sb("botT", [P, BATCH])
        rows = sb("rows", [P, TABLES, DIM])
        featT = sb("featT", [P, P, SLOT])
        pairs = sb("pairs", [P, PAIR_TILES, P])
        index = sb("index", [P, CHUNKS, TABLES], U32)
        pair_index = sb("pair_index", [PAIR_ROWS, PAIR_TILES], U32)

        with ExitStack() as early:
            index_raw = sb("index_raw", [P, CHUNKS, TABLES], I32, early)
            index_tmp = sb("index_tmp", [P, CHUNKS, TABLES], F32, early)
            index_base = sb("index_base", [P, CHUNKS, TABLES], I32, early)
            x0 = sb("x0", [P, CHUNKS, DENSE], F32, early)
            x0T = sb("x0T", [DENSE, BATCH], F32, early)
            v0 = sb("v0", [DENSE, B0], F32, early)
            v1 = sb("v1", [P, B0 // P, B1], F32, early)
            v2 = sb("v2", [P, B1 // P, B2], F32, early)
            c0 = sb("c0", [P, B0 // P], F32, early)
            c1 = sb("c1", [P, B1 // P], F32, early)
            c2 = sb("c2", [P, 1], F32, early)
            h0T = sb("h0T", [P, B0 // P, BATCH], F32, early)
            h1T = sb("h1T", [P, B1 // P, BATCH], F32, early)
        dots = sb("dots", [FEATS, FEATS, P])
        y_evac = sb("y_evac", [P, 2, NB])
        y2T = sb("y2T", [P, T2 // P, P])
        out_row = sb("out_row", [1, P])
        bias1 = sb("bias1", [P, T1])
        bias2 = sb("bias2", [P, T2])
        with ExitStack() as early:
            stage = sb("stage", [P, STAGES, 1024], F32, early)
        xh = sb("xh", [P, PAIR_TILES, P], F32R)
        xl = sb("xl", [P, PAIR_TILES, P], F32R)
        y3T = sb("y3T", [P, T3 // P, P])
        y_split = sb("y_split", [P, 2, 2, NB], F32R)
        yh, yl = y_split[:, :, 0, :], y_split[:, :, 1, :]

        def bank(name):
            return ctx.enter_context(nc.psum_tensor(name, [P, NB], F32))

        acc = [bank("acc0"), bank("acc1"), bank("acc2")]
        turned = [bank("turned0"), bank("turned1")]
        fz = [bank("fz0"), bank("fz1")]
        last = bank("last")

        s_sparse0, s_sparse, s_dense, s_pidx, s_botb, s_topw, s_one = map(
            sem, ("sparse0_in", "sparse_in", "dense_in", "pair_index_in", "bottom_biases_in", "top_small_in", "ones_set"))
        s_v = [sem(f"bottom_weights{i}_in") for i in range(3)]
        s_base, s_ident0, s_ident, s_chain, s_index, s_pad = map(
            sem, ("index_base_set", "ident_zero", "ident_set", "index_chain", "index_ready", "pad_set"))
        s_stage = [sem(f"staged{i}") for i in range(STAGES)]
        s_pair = [sem(f"pair_weights_in{i}") for i in range(PAIR_TILES)]
        s_brow = sem("bias_row_in")
        s_wh, s_wl = sem("weight_hi"), sem("weight_lo")
        s_x0t, s_x0, s_l0b, s_h0, s_l1b, s_h1, s_l2b, s_bot = map(
            sem, ("x0_turned", "x0T_ready", "bot0_done", "h0_ready", "bot1_done", "h1_ready", "bot2_done",
                  "botT_ready"))
        s_gather = [sem(f"gathered{j}") for j in range(LOTS)]
        s_ft, s_fa, s_fd, s_fb = map(sem, ("lot_turned", "lot_copied_act", "lot_copied_dve", "bot_feature_copied"))
        s_z, s_za, s_zd = map(sem, ("dots_done", "dots_copied_act", "dots_copied_dve"))
        s_scr0, s_scr, s_wrap = map(sem, ("scratch_tile0_written", "scratch_rest_written", "scratch_wrap_written"))
        s_pin = [sem(f"pairs{i}_in") for i in range(PAIR_TILES)]
        s_bh, s_bl, s_pre, s_prea, s_pred = map(
            sem, ("bot_hi", "bot_lo", "bot_part_done", "bot_part_copied_act", "bot_part_copied_dve"))
        s_xhp, s_xlp = map(sem, ("pairs_hi", "pairs_lo"))
        s_l = [sem(f"layer{i}_done") for i in range(5)]
        s_e = [sem(f"layer{i}_copied") for i in range(3)]
        s_t = [sem(f"layer{i}_turned") for i in range(3)]
        s_yh = [sem(f"layer{i}_hi") for i in range(2)]
        s_yl = [sem(f"layer{i}_lo") for i in range(2)]
        s_y2, s_y3, s_y4, s_out = map(sem, ("y2T_ready", "y3T_ready", "out_ready", "out_written"))

        def pair_piece(i):
            k = PAIR_ROWS + (i == PAIR_TILES - 1)
            return w0h[0:k, i, :], w0l[0:k, i, :], k

        def w2_piece(k):
            return (w2h[:, k:k + 2, :].rearrange("p k n -> p (k n)"),
                    w2l[:, k:k + 2, :].rearrange("p k n -> p (k n)"), P)

        pieces, sources = [w2_piece(BOT_W.start)], [tw[0][0:P, :]]
        for k in range(T0 // P):
            pieces.append((w1h[:, k, :], w1l[:, k, :], P))
            sources.append(tw[1][k * P:(k + 1) * P, :])
        for k in range(0, T1 // P, 2):
            if k == BOT_W.start:
                pair0 = len(pieces)
                pieces += [pair_piece(i) for i in range(PAIR_TILES)]
                sources += [None] * PAIR_TILES
            pieces.append(w2_piece(k))
            sources.append(tw[2][k * P:(k + 2) * P, :].rearrange("(k p) n -> p k n", p=P))
        w2_tail = pair0 + PAIR_TILES
        total = len(pieces)

        def slot(n):
            return (n - (w2_tail - 1)) % STAGES

        def piece_in(eng, n):
            if sources[n] is None:
                eng.wait_ge(s_pair[n - pair0], 16)
            else:
                on_stage = [m for m in range(n + 1) if slot(m) == slot(n) and sources[m] is not None]
                eng.wait_ge(s_stage[slot(n)], 16 * len(on_stage))
            if n == w2_tail - 1:
                eng.wait_ge(s_brow, 16)

        LATE_PARTS = 2
        part_banks = [acc[2], last, turned[0], turned[1], acc[2], last]

        def bot_part_out(eng, copy, g, done):
            eng.wait_ge(s_pre, g + 1)
            copy(bot_part[:, g // 2, g % 2 * NB:(g % 2 + 1) * NB], part_banks[g][:]).then_inc(done, 1)

        def layer3_bank(c, o):
            return acc[1] if c == CHUNKS - 1 and o == 1 else last

        def layer2_bank(c, half):
            return acc[0] if c >= CHUNKS - 2 and half == 1 else acc[2]

        def dot_quadrant(z, s):
            at = z * GROUP * BANK_GROUPS + s
            to = dots[:, :, at:at + GROUP * (BANK_GROUPS - 1) + 1:GROUP].rearrange("n m g -> n g m")
            block_ = fz[z % 2][SLOT * s:SLOT * s + FEATS, 0:BANK_GROUPS * GROUP * FEATS]
            return to, block_.rearrange("n (g c) -> n g c", g=BANK_GROUPS)[:, :, s * FEATS:(s + 1) * FEATS]

        block = ctx.enter_context(nc.Block())

        @block.sync
        def _(sp):
            sp.dma_start(index_raw[:, 0, :], sparse[0:P, :]).then_inc(s_sparse0, 16)
            sp.dma_start(index_raw[:, 1:, :], sparse[P:, :].rearrange("(c p) t -> p c t", p=P)).then_inc(s_sparse, 16)
            sp.dma_start(x0[:], dense.rearrange("(c p) d -> p c d", p=P)).then_inc(s_dense, 16)
            sp.dma_start(v0[:], bw[0]).then_inc(s_v[0], 16)

            def load_piece(n):
                after(sp, s_wl, n - STAGES + 1)
                dst = stage[:, slot(n), :]
                if len(sources[n].shape) == 3:
                    dst = dst.rearrange("p (k n) -> p k n", k=2)
                sp.dma_start(dst, sources[n]).then_inc(s_stage[slot(n)], 16)

            load_piece(0)
            sp.dma_start(v1[:], bw[1].rearrange("(k p) n -> p k n", p=P)).then_inc(s_v[1], 16)
            load_piece(1)
            sp.dma_start(v2[:], bw[2].rearrange("(k p) n -> p k n", p=P)).then_inc(s_v[2], 16)
            load_piece(2)
            for n in range(STAGES, pair0):
                load_piece(n)
            sp.wait_ge(s_wl, w2_tail - STAGES)
            sp.dma_start(stage[PAIR_ROWS:PAIR_ROWS + 1, slot(w2_tail - 1), :],
                         tb[0].rearrange("(o n) -> o n", o=1)).then_inc(s_brow, 16)

            def load_upper():
                sp.dma_start(w3[:], tw[3].rearrange("(k p) n -> p k n", p=P)).then_inc(s_topw, 16)
                sp.dma_start(w4[:], tw[4].rearrange("(k p) n -> p (k n)", p=P), allow_slow_non_contiguous=True).then_inc(s_topw, 16)
                sp.wait_ge(s_bot, 1)
                sp.dma_start(bias1[:], flat(tb[1], 0, [[0, P], [1, T1]])).then_inc(s_topw, 16)
                sp.dma_start(bias2[:], flat(tb[2], 0, [[0, P], [1, T2]])).then_inc(s_topw, 16)

            def regroup(c):
                sp.wait_ge(s_za, Z_BANKS * (c + 1))
                sp.wait_ge(s_zd, Z_BANKS * (c + 1))
                for i in range(PAIR_TILES):
                    after(sp, s_pin[i], 16 * c)
                sp.dma_start(scratch[0:TILE_FEATS, 0:FEATS, :], dots[0:TILE_FEATS]).then_inc(s_scr0, 16)
                sp.dma_start(scratch[TILE_FEATS:, 0:FEATS, :], dots[TILE_FEATS:]).then_inc(s_scr, 16)
                sp.dma_start(scratch[:, FEATS:WRAP, :], dots[:, 0:HOPS, :]).then_inc(s_wrap, 16)
                after(sp, s_xlp, PAIR_TILES * c)
                if c == 0:
                    sp.wait_ge(s_one, 1)
                for i in range(PAIR_TILES):
                    if i == 0:
                        sp.wait_ge(s_scr0, 16 * (c + 1))
                    elif i == 1:
                        sp.wait_ge(s_scr, 16 * (c + 1))
                        sp.wait_ge(s_wrap, 16 * (c + 1))
                    src = flat(scratch, (i * TILE_FEATS * (WRAP + 1) + 1) * P,
                               [[(WRAP + 1) * P, TILE_FEATS], [P, HOPS], [1, P]])
                    sp.dma_start(pairs[0:PAIR_ROWS, i, :], src).then_inc(s_pin[i], 16)
                    if c == 0 and i == 0:
                        load_piece(w2_tail)

            def write_out(c):
                sp.wait_ge(s_y4, c + 1)
                sp.dma_start(out.rearrange("b o -> o b")[:, c * P:(c + 1) * P], out_row[:]).then_inc(s_out, 16)

            for c in range(CHUNKS):
                regroup(c)
                if c == 0:
                    for n in range(w2_tail + 1, total):
                        load_piece(n)
                    load_upper()
                else:
                    write_out(c - 1)
            write_out(CHUNKS - 1)
            sp.wait_ge(s_out, 16 * CHUNKS)

        @block.gpsimd
        def _(pool):
            pool.iota(index_base[:], pattern=[[0, CHUNKS], [VOCAB, TABLES]], base=0,
                      channel_multiplier=0).then_inc(s_base, 1)
            pool.memset(ident[:], 0.0).then_inc(s_ident0, 1)
            pool.wait_ge(s_ident0, 1)
            pool.affine_select(out=ident[:], in_=ident[:], compare_op=ALU.not_equal, fill=1.0, base=0,
                               pattern=[[-1, P]], channel_multiplier=1).then_inc(s_ident, 1)
            table = emb.rearrange("t v d -> (t v) d")

            def gather_lot(c, j):
                after(pool, s_ft, LOTS * (c - 1) + j + 1)
                for t in range(LOT * j, min(LOT * (j + 1), TABLES)):
                    pool.indirect_dma_start(
                        rows[:, t, :], None, table,
                        bass.IndirectOffsetOnAxis(ap=index[:, c, t:t + 1], axis=0)).then_inc(s_gather[j], 16)

            pool.wait_ge(s_index, 1)
            for j in range(LOTS):
                gather_lot(0, j)
            pool.wait_ge(s_index, 2)
            gather_lot(1, 0)
            pool.wait_ge(s_pidx, 16)
            for i in range(PAIR_TILES):
                n = pair0 + i
                pool.wait_ge(s_wl, n - STAGES + 1)
                pool.indirect_dma_start(
                    stage[0:PAIR_ROWS, slot(n), :], None, tw[0],
                    bass.IndirectOffsetOnAxis(ap=pair_index[:, i:i + 1], axis=0)).then_inc(s_pair[i], 16)
            for j in range(1, LOTS):
                gather_lot(1, j)
            for c in range(2, CHUNKS):
                for j in range(LOTS):
                    gather_lot(c, j)

        @block.scalar
        def _(act):
            act.dma_start(c0[:], bb[0].rearrange("(k p) -> p k", p=P), allow_slow_non_contiguous=True).then_inc(s_botb, 16)
            act.dma_start(c1[:], bb[1].rearrange("(k p) -> p k", p=P), allow_slow_non_contiguous=True).then_inc(s_botb, 16)
            act.dma_start(c2[:], bb[2].rearrange("(k p) -> p k", p=P), allow_slow_non_contiguous=True).then_inc(s_botb, 16)
            act.dma_start(pair_index[:], pair_rows).then_inc(s_pidx, 16)
            act.dma_start(bias3[:], tb[3].rearrange("(k p) -> p k", p=P), allow_slow_non_contiguous=True).then_inc(s_topw, 16)
            act.dma_start(bias4[:], tb[4].rearrange("(o n) -> o n", o=1)).then_inc(s_topw, 16)

            def weight_hi(n):
                hi, _, k = pieces[n]
                piece_in(act, n)
                nc.scalar.copy(hi, stage[0:k, slot(n), :]).then_inc(s_wh, 1)

            def feature_lot(c, j):
                act.wait_ge(s_ft, LOTS * c + j + 1)
                w = min(LOT, TABLES - LOT * j)
                nc.scalar.copy(
                    featT[:, :, 1 + LOT * j:1 + LOT * j + w].rearrange("d b n -> d n b"),
                    fz[j % 2][:, 0:w * P].rearrange("d (n b) -> d n b", b=P)).then_inc(s_fa, 1)

            def dots_out(c):
                after(act, s_scr0, 16 * c)
                after(act, s_scr, 16 * c)
                after(act, s_wrap, 16 * c)
                for z in range(Z_BANKS):
                    act.wait_ge(s_z, Z_BANKS * c + z + 1)
                    for s in (0, 1):
                        ins = nc.scalar.copy(*dot_quadrant(z, s))
                    ins.then_inc(s_za, 1)

            def split_hi(layer, c, half):
                act.wait_ge(s_t[layer], 2 * c + half + 1)
                nc.scalar.activation(yh[:, half, :], turned[half][:], ACT.Relu).then_inc(s_yh[layer], 1)

            def pairs_hi(c, i):
                act.wait_ge(s_pin[i], 16 * (c + 1))
                after(act, s_l[0], 2 * c)
                nc.scalar.copy(xh[0:PAIR_ROWS + 1, i, :], pairs[0:PAIR_ROWS + 1, i, :]).then_inc(s_xhp, 1)

            def layer2_out(c, half):
                act.wait_ge(s_t[2], 2 * c + half + 1)
                nc.scalar.activation(y2T[:, 2 * half:2 * half + 2, :].rearrange("p k b -> p (k b)"),
                                     turned[half][:, 0:T2 // 2], ACT.Relu).then_inc(s_y2, 1)

            def layer3_out(c):
                for o in range(T3 // P):
                    done = o + 1 if c == CHUNKS - 1 else T3 // P
                    act.wait_ge(s_l[3], T3 // P * c + done)
                    nc.scalar.activation(y3T[:, o, :], layer3_bank(c, o)[:, o * P:(o + 1) * P], ACT.Relu,
                                         bias=bias3[:, o:o + 1]).then_inc(s_y3, 1)

            def layer4_out(c):
                act.wait_ge(s_l[4], c + 1)
                after(act, s_out, 16 * c)
                nc.scalar.activation(out_row[:], last[0:1, T3:T3 + P], ACT.Relu,
                                     bias=bias4[:]).then_inc(s_y4, 1)

            def bottom0(o):
                act.wait_ge(s_l0b, o + 1)
                nc.scalar.activation(h0T[:, o, :], (acc + [last])[o][:], ACT.Relu,
                                     bias=c0[:, o:o + 1]).then_inc(s_h0, 1)

            def bottom1(o):
                act.wait_ge(s_l1b, o + 1)
                nc.scalar.activation(h1T[:, o, :], turned[o][:], ACT.Relu, bias=c1[:, o:o + 1]).then_inc(s_h1, 1)

            def bottom2():
                act.wait_ge(s_l2b, 1)
                nc.scalar.activation(botT[:], acc[0][:], ACT.Relu, bias=c2[:]).then_inc(s_bot, 1)
                act.wait_ge(s_bot, 1)
                nc.scalar.copy(w2h[:, BOT_X, :], botT[:]).then_inc(s_bh, 1)

            act.wait_ge(s_botb, 3 * 16)
            act.wait_ge(s_pad, 1)
            weight_hi(0)
            bottom0(0)
            bottom0(1)
            weight_hi(1)
            bottom0(2)
            weight_hi(2)
            bottom0(3)
            feature_lot(0, 0)
            for n in (3, 4, 5):
                weight_hi(n)
            bottom1(0)
            weight_hi(6)
            bottom1(1)
            feature_lot(0, 2)
            weight_hi(7)
            bottom2()
            weight_hi(8)
            bot_part_out(act, nc.scalar.copy, 0, s_prea)
            weight_hi(9)
            feature_lot(0, 4)
            weight_hi(10)
            feature_lot(0, 6)

            def chunk(c):
                first = c == 0
                end = c == CHUNKS - 1
                dots_out(c)
                if first:
                    for n in range(pair0, w2_tail):
                        weight_hi(n)
                    for g in range(LATE_PARTS, 2 * (CHUNKS - 1), 2):
                        bot_part_out(act, nc.scalar.copy, g, s_prea)
                    act.wait_ge(s_wl, w2_tail)
                    feature_lot(c + 1, 0)
                    for i in range(PAIR_TILES):
                        pairs_hi(c, i)
                    act.wait_ge(s_pre, 2 * (CHUNKS - 1))
                    weight_hi(w2_tail)
                    act.wait_ge(s_l[0], 1)
                    nc.scalar.copy(y_evac[:, 0, :], acc[0][:]).then_inc(s_e[0], 1)
                    act.wait_ge(s_wl, w2_tail + 1)
                else:
                    split_hi(1, c - 1, 1)
                    pairs_hi(c, 0)
                    pairs_hi(c, 1)
                    layer2_out(c - 1, 0)
                    layer2_out(c - 1, 1)
                    pairs_hi(c, 2)
                    if not end:
                        feature_lot(c + 1, 0)
                    layer3_out(c - 1)
                    layer4_out(c - 1)
                split_hi(0, c, 0)
                if first:
                    weight_hi(total - 1)
                if not end:
                    feature_lot(c + 1, 2)
                if first:
                    act.wait_ge(s_wl, total)
                split_hi(0, c, 1)
                if not end:
                    for j in range(4, LOTS, 2):
                        feature_lot(c + 1, j)
                split_hi(1, c, 0)

            for c in range(CHUNKS):
                chunk(c)
            split_hi(1, CHUNKS - 1, 1)
            layer2_out(CHUNKS - 1, 0)
            layer2_out(CHUNKS - 1, 1)
            layer3_out(CHUNKS - 1)
            layer4_out(CHUNKS - 1)

        @block.vector
        def _(dve):
            nc.vector.memset(featT[:, :, FEATS:SLOT], 0.0).then_inc(s_pad, 1)
            nc.vector.memset(pairs[96:P, :, :], 1.0).then_inc(s_one, 1)

            def indices(chunks, done):
                raw, tmp = index_raw[:, chunks, :], index_tmp[:, chunks, :]
                nc.vector.tensor_scalar(tmp, raw, 0.0, float(VOCAB), ALU.is_lt, ALU.mult).then_inc(s_chain, 1)
                dve.wait_ge(s_chain, done + 1)
                nc.vector.tensor_tensor(tmp, tmp, raw, ALU.add).then_inc(s_chain, 1)
                dve.wait_ge(s_chain, done + 2)
                nc.vector.tensor_scalar(tmp, tmp, 0.0, float(VOCAB - 1), ALU.max, ALU.min).then_inc(s_chain, 1)
                dve.wait_ge(s_chain, done + 3)
                nc.vector.tensor_tensor(index[:, chunks, :], tmp, index_base[:, chunks, :],
                                        ALU.add).then_inc(s_index, 1)

            dve.wait_ge(s_sparse0, 16)
            dve.wait_ge(s_base, 1)
            indices(slice(0, 1), 0)

            def weight_lo(n):
                hi, lo, k = pieces[n]
                dve.wait_ge(s_wh, n + 1)
                nc.vector.tensor_tensor(lo, stage[0:k, slot(n), :], hi.bitcast(F32),
                                        ALU.subtract).then_inc(s_wl, 1)

            def feature_lot(c, j):
                dve.wait_ge(s_ft, LOTS * c + j + 1)
                nc.vector.tensor_copy(
                    featT[:, :, 1 + LOT * j:1 + LOT * (j + 1)].rearrange("d b n -> d n b"),
                    fz[j % 2][:].rearrange("d (n b) -> d n b", b=P)).then_inc(s_fd, 1)

            def bot_feature(c):
                dve.wait_ge(s_ft, LOTS * c + 1)
                nc.vector.tensor_copy(featT[:, :, 0], botT[:, c * P:(c + 1) * P]).then_inc(s_fb, 1)

            def dots_out(c):
                after(dve, s_scr0, 16 * c)
                after(dve, s_scr, 16 * c)
                after(dve, s_wrap, 16 * c)
                for z in range(Z_BANKS):
                    dve.wait_ge(s_z, Z_BANKS * c + z + 1)
                    for s in (2, 3):
                        ins = nc.vector.tensor_copy(*dot_quadrant(z, s))
                    ins.then_inc(s_zd, 1)

            def pairs_lo(c):
                for i in range(PAIR_TILES):
                    dve.wait_ge(s_xhp, PAIR_TILES * c + i + 1)
                    nc.vector.tensor_tensor(xl[0:PAIR_ROWS + 1, i, :], pairs[0:PAIR_ROWS + 1, i, :],
                                            xh[0:PAIR_ROWS + 1, i, :].bitcast(F32),
                                            ALU.subtract).then_inc(s_xlp, 1)

            def copy_out(layer, c, half):
                if layer == 2:
                    dve.wait_ge(s_l[2], 2 * c + half + 1)
                    cols = slice(half * T2 // 2, (half + 1) * T2 // 2)
                    nc.vector.tensor_tensor(y_evac[:, 0, cols], layer2_bank(c, half)[:, cols], bias2[:, cols],
                                            ALU.add).then_inc(s_e[2], 1)
                    return
                dve.wait_ge(s_l[layer], 2 * c + half + 1)
                if layer == 0 and c > 0:
                    ins = nc.vector.tensor_tensor(y_evac[:, half, :], acc[half][:],
                                                  bot_part[:, c - 1, half * NB:(half + 1) * NB], ALU.add)
                elif layer == 0:
                    ins = nc.vector.tensor_copy(y_evac[:, half, :], acc[half][:])
                else:
                    ins = nc.vector.tensor_tensor(y_evac[:, half, :], acc[half][:],
                                                  bias1[:, half * NB:(half + 1) * NB], ALU.add)
                ins.then_inc(s_e[layer], 1)

            def split_lo(layer, c, half):
                if layer == 0 and c == 0:
                    dve.wait_ge(s_wl, w2_tail + 1 + half)
                dve.wait_ge(s_yh[layer], 2 * c + half + 1)
                nc.vector.scalar_tensor_tensor(out=yl[:, half, :], in0=turned[half][:], scalar=0.0,
                                               in1=yh[:, half, :].bitcast(F32), op0=ALU.max,
                                               op1=ALU.subtract).then_inc(s_yl[layer], 1)

            dve.wait_ge(s_x0t, 1)
            nc.vector.tensor_copy(x0T[:], turned[1][0:DENSE, :]).then_inc(s_x0, 1)
            dve.wait_ge(s_sparse, 16)
            indices(slice(1, CHUNKS), 3)
            for n in range(5):
                weight_lo(n)
            feature_lot(0, 1)
            for n in range(5, 8):
                weight_lo(n)
            dve.wait_ge(s_bh, 1)
            nc.vector.tensor_tensor(w2l[:, BOT_X, :], botT[:], w2h[:, BOT_X, :].bitcast(F32),
                                    ALU.subtract).then_inc(s_bl, 1)
            feature_lot(0, 3)
            bot_feature(0)
            weight_lo(8)
            bot_part_out(dve, nc.vector.tensor_copy, 1, s_pred)
            weight_lo(9)
            feature_lot(0, 5)
            weight_lo(10)

            def chunk(c):
                first = c == 0
                end = c == CHUNKS - 1
                dots_out(c)
                if first:
                    for n in range(pair0, w2_tail):
                        weight_lo(n)
                    for g in range(LATE_PARTS + 1, 2 * (CHUNKS - 1), 2):
                        bot_part_out(dve, nc.vector.tensor_copy, g, s_pred)
                else:
                    split_lo(1, c - 1, 1)
                    copy_out(2, c - 1, 0)
                    copy_out(2, c - 1, 1)
                pairs_lo(c)
                if first:
                    weight_lo(w2_tail)
                if not end:
                    feature_lot(c + 1, 1)
                if not first:
                    copy_out(0, c, 0)
                split_lo(0, c, 0)
                copy_out(0, c, 1)
                if first:
                    weight_lo(total - 1)
                if not end:
                    feature_lot(c + 1, 3)
                split_lo(0, c, 1)
                if not end:
                    for j in range(5, LOTS, 2):
                        feature_lot(c + 1, j)
                    bot_feature(c + 1)
                copy_out(1, c, 0)
                split_lo(1, c, 0)
                copy_out(1, c, 1)

            for c in range(CHUNKS):
                chunk(c)
            split_lo(1, CHUNKS - 1, 1)
            copy_out(2, CHUNKS - 1, 0)
            copy_out(2, CHUNKS - 1, 1)

        @block.tensor
        def _(pe):
            def turn_lot(c, j):
                w = min(LOT, TABLES - LOT * j)
                pe.wait_ge(s_gather[j], 16 * w * (c + 1))
                if j < 2:
                    after(pe, s_za, Z_BANKS * c)
                    after(pe, s_zd, Z_BANKS * c)
                elif j % 2 == 0:
                    pe.wait_ge(s_fa, ACT_LOTS * c + j // 2)
                else:
                    pe.wait_ge(s_fd, DVE_LOTS * c + j // 2)
                for i in range(w):
                    ins = nc.tensor.transpose(fz[j % 2][:, i * P:(i + 1) * P], rows[:, LOT * j + i, :], ident[:])
                ins.then_inc(s_ft, 1)

            def dots_of(c):
                pe.wait_ge(s_fa, ACT_LOTS * (c + 1))
                pe.wait_ge(s_fd, DVE_LOTS * (c + 1))
                pe.wait_ge(s_fb, c + 1)
                for z in range(Z_BANKS):
                    if z >= 2:
                        pe.wait_ge(s_za, Z_BANKS * c + z - 1)
                        pe.wait_ge(s_zd, Z_BANKS * c + z - 1)
                    for g in range(BANK_GROUPS):
                        b = (z * BANK_GROUPS + g) * GROUP
                        w = GROUP * FEATS
                        w_rows = (GROUP - 1) * SLOT + FEATS
                        ins = nc.tensor.matmul(
                            fz[z % 2][0:w_rows, g * w:(g + 1) * w].rearrange("n (s m) -> n s m", s=GROUP),
                            featT[:, b:b + GROUP, :].rearrange("d s n -> d (s n)")[:, 0:w_rows],
                            featT[:, b:b + GROUP, 0:FEATS], start=True, stop=True)
                    ins.then_inc(s_z, 1)

            def product(dst, ah, al, wh, wl, first, end, lo_ready=None):
                nc.tensor.matmul(dst, ah, wh, start=first, stop=False)
                nc.tensor.matmul(dst, ah, wl, start=False, stop=False)
                if lo_ready is not None:
                    pe.wait_ge(*lo_ready)
                return nc.tensor.matmul(dst, al, wh, start=False, stop=end)

            def bot_times_w0(dst, c, half):
                at = slice(c * P, (c + 1) * P)
                return product(dst[:], w2h[:, BOT_X, at], w2l[:, BOT_X, at], w0bot(w2h, half), w0bot(w2l, half),
                               True, c > 0)

            def w0bot(w, half):
                return w[:, BOT_W, :].rearrange("p k n -> p (k n)")[:, half * NB:(half + 1) * NB]

            def layer0(c, half, k, end=False):
                if half == 0:
                    pe.wait_ge(s_xhp, PAIR_TILES * c + k + 1)
                lo_ready = (s_xlp, PAIR_TILES * c + k + 1) if half == 0 else None
                n = PAIR_ROWS + (k == PAIR_TILES - 1)
                cols = slice(half * NB, (half + 1) * NB)
                ins = product(acc[half][:], xh[0:n, k, :], xl[0:n, k, :], w0h[0:n, k, cols], w0l[0:n, k, cols],
                              k == 0 and c > 0, end, lo_ready)
                if end:
                    ins.then_inc(s_l[0], 1)

            def upper(layer, half, k, lo_ready=None):
                wh, wl, dst = (w1h, w1l, acc[half]) if layer == 1 else (w2h, w2l, acc[2])
                cols = slice(half * NB, (half + 1) * NB)
                src, at = k // 4, slice((k % 4) * P, (k % 4 + 1) * P)
                ins = product(dst[:], yh[:, src, at], yl[:, src, at], wh[:, k, cols], wl[:, k, cols],
                              k == 0, k == T0 // P - 1, lo_ready)
                if k == T0 // P - 1:
                    ins.then_inc(s_l[layer], layer)

            def layer2_half(c, half, k, lo_ready=None):
                cols = slice(half * T2 // 2, (half + 1) * T2 // 2)
                src, at = k // 4, slice((k % 4) * P, (k % 4 + 1) * P)
                ins = product(layer2_bank(c, half)[:, cols], yh[:, src, at], yl[:, src, at],
                              w2h[:, k, cols], w2l[:, k, cols], k == 0, k == T1 // P - 1, lo_ready)
                if k == T1 // P - 1:
                    ins.then_inc(s_l[2], 1)

            def turn(layer, c, half):
                pe.wait_ge(s_e[layer], 2 * c + half + 1)
                if layer == 0 and c == 0 and half == 0:
                    pe.wait_ge(s_prea, CHUNKS - 1)
                    pe.wait_ge(s_pred, CHUNKS - 1)
                elif layer == 0 and half == 0:
                    after(pe, s_y2, 2 * c)
                for i in range(NB // P):
                    ins = nc.tensor.transpose(turned[half][:, i * P:(i + 1) * P],
                                              y_evac[:, half, i * P:(i + 1) * P], ident[:])
                ins.then_inc(s_t[layer], 1)

            def hi_ready(layer, c, half):
                pe.wait_ge(s_yh[layer], 2 * c + half + 1)
                return s_yl[layer], 2 * c + half + 1

            def turn2(c, half):
                pe.wait_ge(s_e[2], 2 * c + half + 1)
                for i in range(2):
                    at = (2 * half + i) * P
                    ins = nc.tensor.transpose(turned[half][:, i * P:(i + 1) * P],
                                              y_evac[:, 0, at:at + P], ident[:])
                ins.then_inc(s_t[2], 1)

            def layer2(c):
                upper(2, 0, 0, hi_ready(1, c, 0))
                turn(1, c, 1)
                for k in range(1, 4):
                    upper(2, 0, k)
                for k in range(4, 8):
                    upper(2, 0, k, hi_ready(1, c, 1) if k == 4 else None)

            def layer2_in_halves(c):
                layer2_half(c, 0, 0, hi_ready(1, c, 0))
                layer2_half(c, 1, 0)
                turn(1, c, 1)
                for half in range(2):
                    for k in range(1, 4):
                        layer2_half(c, half, k)
                for half in range(2):
                    for k in range(4, 8):
                        layer2_half(c, half, k, hi_ready(1, c, 1) if (half, k) == (0, 4) else None)
                turn2(c, 0)
                turn2(c, 1)

            def layer3(c):
                pe.wait_ge(s_y2, 2 * c + 2)
                after(pe, s_y4, c)
                for o in range(T3 // P):
                    for k in range(T2 // P):
                        layer3_tile(c, o, k)

            def layer3_in_turns(c):
                after(pe, s_y4, c)
                for half in range(2):
                    pe.wait_ge(s_y2, 2 * c + half + 1)
                    for o in range(T3 // P):
                        for k in (2 * half, 2 * half + 1):
                            layer3_tile(c, o, k)

            def layer3_tile(c, o, k):
                at = slice(o * P, (o + 1) * P)
                ins = nc.tensor.matmul(layer3_bank(c, o)[:, at], w3[:, k, at], y2T[:, k, :],
                                       start=(k == 0), stop=(k == T2 // P - 1))
                if k == T2 // P - 1:
                    ins.then_inc(s_l[3], 1)

            def layer4(c):
                for k in range(T3 // P):
                    done = k + 1 if c == CHUNKS - 1 else T3 // P
                    pe.wait_ge(s_y3, T3 // P * c + done)
                    ins = nc.tensor.matmul(last[0:1, T3:T3 + P], w4[:, k:k + 1], y3T[:, k, :],
                                           start=(k == 0), stop=(k == T3 // P - 1))
                ins.then_inc(s_l[4], 1)

            pe.wait_ge(s_ident, 1)
            pe.wait_ge(s_dense, 16)
            for c in range(CHUNKS):
                ins = nc.tensor.transpose(turned[1][0:DENSE, c * P:(c + 1) * P], x0[:, c, :], ident[:])
            ins.then_inc(s_x0t, 1)
            pe.wait_ge(s_v[0], 16)
            pe.wait_ge(s_x0, 1)
            for o in range(B0 // P):
                nc.tensor.matmul((acc + [last])[o][:], v0[:, o * P:(o + 1) * P], x0T[:], start=True,
                                 stop=True).then_inc(s_l0b, 1)
            turn_lot(0, 0)
            pe.wait_ge(s_v[1], 16)
            for k in range(B0 // P):
                if k == 2:
                    turn_lot(0, 1)
                pe.wait_ge(s_h0, k + 1)
                for o in range(B1 // P):
                    ins = nc.tensor.matmul(turned[o][:], v1[:, k, o * P:(o + 1) * P], h0T[:, k, :],
                                           start=(k == 0), stop=(k == B0 // P - 1))
                    if k == B0 // P - 1:
                        ins.then_inc(s_l1b, 1)
            turn_lot(0, 2)
            pe.wait_ge(s_v[2], 16)
            for k in range(B1 // P):
                pe.wait_ge(s_h1, k + 1)
                ins = nc.tensor.matmul(acc[0][:], v2[:, k, :], h1T[:, k, :], start=(k == 0),
                                       stop=(k == B1 // P - 1))
            ins.then_inc(s_l2b, 1)
            turn_lot(0, 3)
            pe.wait_ge(s_wl, 1)
            pe.wait_ge(s_bh, 1)
            pe.wait_ge(s_bl, 1)
            for g in range(LATE_PARTS):
                bot_times_w0(part_banks[g], g // 2 + 1, g % 2).then_inc(s_pre, 1)
            turn_lot(0, 4)
            for half in range(2):
                bot_times_w0(acc[half], 0, half)
            turn_lot(0, 5)
            turn_lot(0, 6)

            def chunk(c):
                first = c == 0
                end = c == CHUNKS - 1
                dots_of(c)
                if end:
                    layer2_in_halves(c - 1)
                elif not first:
                    layer2(c - 1)
                if not end:
                    turn_lot(c + 1, 0)
                if first:
                    pe.wait_ge(s_prea, LATE_PARTS // 2)
                    pe.wait_ge(s_pred, LATE_PARTS // 2)
                    for g in range(LATE_PARTS, 2 * (CHUNKS - 1)):
                        bot_times_w0(part_banks[g], g // 2 + 1, g % 2).then_inc(s_pre, 1)
                    turn_lot(c + 1, 1)
                    pe.wait_ge(s_wl, w2_tail)
                else:
                    if not end:
                        turn_lot(c + 1, 1)
                        turn2(c - 1, 0)
                        turn2(c - 1, 1)
                layer0(c, 0, 0)
                if first:
                    layer0(c, 1, 0)
                layer0(c, 0, 1)
                if not first:
                    layer3(c - 1)
                layer0(c, 0, 2, end=True)
                if not first:
                    layer0(c, 1, 0)
                    layer4(c - 1)
                if not end:
                    turn_lot(c + 1, 2)
                turn(0, c, 0)
                layer0(c, 1, 1)
                layer0(c, 1, 2, end=True)
                if not end and not first:
                    turn_lot(c + 1, 3)
                upper(1, 0, 0, hi_ready(0, c, 0))
                upper(1, 0, 1)
                turn(0, c, 1)
                if first:
                    turn_lot(c + 1, 3)
                    pe.wait_ge(s_wl, total)
                    pe.wait_ge(s_topw, 6 * 16)
                steps = [(0, 2), (0, 3), (1, 0), (1, 1), (1, 2), (1, 3), (0, 4), (0, 5), (0, 6), (0, 7)]
                lots = {(1, 3): 4, (0, 6): 5}
                for half, k in steps:
                    upper(1, half, k, hi_ready(0, c, 1) if (half, k) == (0, 4) else None)
                    if (half, k) in lots and not end:
                        turn_lot(c + 1, lots[half, k])
                upper(1, 1, 4)
                upper(1, 1, 5)
                if not end:
                    turn_lot(c + 1, 6)
                turn(1, c, 0)
                upper(1, 1, 6)
                upper(1, 1, 7)

            for c in range(CHUNKS):
                chunk(c)
            layer2_in_halves(CHUNKS - 1)
            layer3_in_turns(CHUNKS - 1)
            layer4(CHUNKS - 1)


_BOT = [("L0_rec_bw%d" % i, "L0_rec_bb%d" % i) for i in range(3)]
_TOP = [("L0_rec_tw%d" % i, "L0_rec_tb%d" % i) for i in range(5)]
_INS = ["r_dense_x", "r_sparse_x", "L0_rec_emb"] + [n for pair in _BOT + _TOP for n in pair]


def kernel(**inputs):
    import concourse.bacc as bacc
    from concourse.bass_utils import run_bass_kernel_spmd as run

    nc = bacc.Bacc("TRN2", target_bir_lowering=False, num_devices=1)
    arrays, aps = {}, {}
    for name in _INS:
        a = np.ascontiguousarray(inputs[name])
        arrays["in_" + name] = a
        aps[name] = nc.dram_tensor("in_" + name, a.shape, mybir.dt.from_np(a.dtype), kind="ExternalInput").ap()
    arrays["pair_rows"] = pair_row_table()
    pair_rows = nc.dram_tensor("pair_rows", (PAIR_ROWS, PAIR_TILES), U32, kind="ExternalInput").ap()
    scratch = nc.dram_tensor("pair_scratch", (FEATS, WRAP, P), F32, kind="Internal").ap()
    out = nc.dram_tensor("out_y", (BATCH, 1), F32, kind="ExternalOutput").ap()
    rec_kernel(nc, aps["r_dense_x"], aps["r_sparse_x"], aps["L0_rec_emb"],
               [aps[w] for w, _ in _BOT], [aps[b] for _, b in _BOT],
               [aps[w] for w, _ in _TOP], [aps[b] for _, b in _TOP], pair_rows, scratch, out)
    result = run(nc, [arrays], core_ids=[0])
    return result.results[0]["out_y"]
```
